# Optimizing a Trainium2 kernel written in Bass

```python
import numpy as np
import jax
import jax.numpy as jnp

def _softmax(x, axis=-1):
    return jax.nn.softmax(x, axis=axis)
def _gelu(x):
    return jax.nn.gelu(x, approximate=True)
def _silu(x):
    return jax.nn.silu(x)
def _sigmoid(x):
    return jax.nn.sigmoid(x)
def _layernorm(x, axis=-1, eps=1e-5):
    m = jnp.mean(x, axis=axis, keepdims=True)
    v = jnp.var(x, axis=axis, keepdims=True)
    return (x - m) / jnp.sqrt(v + eps)
def _scatter_add(tgt, idx, src, axis=0):
    return tgt.at[idx].add(src)
def _segment_sum(src, seg, n):
    return jax.ops.segment_sum(src, seg, n)

kernel_name = 'mk_adj_preln_d2_adj_256_64c5e9'

def setup_inputs(seed: int = 0):
    np.random.seed(seed)
    _w = jnp.asarray
    def _rec_inputs():
        import jax
        import jax.numpy as jnp
        _gk = jax.random.key(seed)
        x = -0.0002928 + 1 * jax.random.normal(jax.random.fold_in(_gk, 1), (8, 2048, 256), jnp.float32)
        _w = (1.0 + jnp.arange(2048, dtype=jnp.float32)) ** -0.5
        _w = _w / _w.mean()
        _pij = jnp.clip(0.00195312 * _w[:, None] * _w[None, :], 0.0, 1.0)
        _a = jax.random.uniform(jax.random.fold_in(_gk, 2), (8, 2048, 2048)) < _pij
        adj = _a.astype(jnp.int32)
        return x, adj
    x, adj = _rec_inputs()
    def _L0_gnn_setup():
        import jax, jax.numpy as jnp
        import numpy as np
        NEG_INF = -1000000000.0
        LEAKY_SLOPE = 0.2
        key = jax.random.key(seed)
        k1, k2, k3, k4, k5 = jax.random.split(key, 5)
        B, N, F_in, F_out = (8, 2048, 256, 256)
        x = jax.random.normal(k1, (B, N, F_in), dtype=jnp.float32)
        adj = jax.random.randint(k2, (B, N, N), 0, 2, dtype=jnp.int32)
        W = jax.random.normal(k3, (F_out, F_in), dtype=jnp.float32) * 0.05
        a_src = jax.random.normal(k4, (F_out,), dtype=jnp.float32) * 0.05
        a_dst = jax.random.normal(k5, (F_out,), dtype=jnp.float32) * 0.05
        return {'x': x, 'adj': adj, 'W': W, 'a_src': a_src, 'a_dst': a_dst}
    _L0_gnn_all = _L0_gnn_setup()
    _L0_gnn_in = {k: v for k, v in _L0_gnn_all.items() if k in ('W', 'a_src', 'a_dst', )}
    del _L0_gnn_all

    def _L1_gnn_setup():
        import jax, jax.numpy as jnp
        import numpy as np
        NEG_INF = -9000000000000000.0
        ALPHA = 0.2
        key = jax.random.key(seed)
        k1, k2, k3, k4 = jax.random.split(key, 4)
        B, N, C_IN, C_OUT, H = (8, 2048, 256, 256, 4)
        node_feats = jax.random.normal(k1, (B, N, C_IN), dtype=jnp.float32)
        adj_matrix = jax.random.randint(k2, (B, N, N), 0, 2, dtype=jnp.int32)
        eye = jnp.eye(N, dtype=jnp.int32)[None]
        adj_matrix = jnp.maximum(adj_matrix, eye)
        W = jax.random.normal(k3, (C_OUT, C_IN), dtype=jnp.float32) * (1.414 / np.sqrt(C_IN))
        b = jnp.zeros((C_OUT,), dtype=jnp.float32)
        a = jax.random.normal(k4, (H, 2 * (C_OUT // H)), dtype=jnp.float32) * 0.1
        return {'node_feats': node_feats, 'adj_matrix': adj_matrix, 'W': W, 'b': b, 'a': a}
    _L1_gnn_all = _L1_gnn_setup()
    _L1_gnn_in = {k: v for k, v in _L1_gnn_all.items() if k in ('W', 'b', 'a', )}
    del _L1_gnn_all

    return {
        "x": x,
        "adj": adj,
        "L0_gnn_W": _L0_gnn_in["W"],
        "L0_gnn_a_src": _L0_gnn_in["a_src"],
        "L0_gnn_a_dst": _L0_gnn_in["a_dst"],
        "L1_gnn_W": _L1_gnn_in["W"],
        "L1_gnn_b": _L1_gnn_in["b"],
        "L1_gnn_a": _L1_gnn_in["a"],
    }

def reference(x, adj, L0_gnn_W, L0_gnn_a_src, L0_gnn_a_dst, L1_gnn_W, L1_gnn_b, L1_gnn_a):
    import jax
    import jax.numpy as jnp
    def _L0_gnn_ref(x, adj, W, a_src, a_dst):
        import jax, jax.numpy as jnp
        import numpy as np
        NEG_INF = -1000000000.0
        LEAKY_SLOPE = 0.2
        h = jnp.einsum('bnf,of->bno', x, W)
        s_src = h @ a_src
        s_dst = h @ a_dst
        e = s_src[:, :, None] + s_dst[:, None, :]
        e = jax.nn.leaky_relu(e, negative_slope=LEAKY_SLOPE)
        e = jnp.where(adj == 0, jnp.float32(NEG_INF), e)
        alpha = jax.nn.softmax(e, axis=-1)
        h_prime = jnp.einsum('bij,bjo->bio', alpha, h)
        return h_prime

    def _L1_gnn_ref(node_feats, adj_matrix, W, b, a):
        import jax, jax.numpy as jnp
        import numpy as np
        NEG_INF = -9000000000000000.0
        ALPHA = 0.2
        B, N, _ = node_feats.shape
        H, two_c = a.shape
        c = two_c // 2
        f = (jnp.einsum('bni,oi->bno', node_feats, W) + b).reshape(B, N, H, c)
        a_src, a_dst = (a[:, :c], a[:, c:])
        s_src = jnp.einsum('bnhc,hc->bnh', f, a_src)
        s_dst = jnp.einsum('bnhc,hc->bnh', f, a_dst)
        logits = jax.nn.leaky_relu(s_src[:, :, None, :] + s_dst[:, None, :, :], ALPHA)
        logits = jnp.where(adj_matrix[..., None] == 1, logits, NEG_INF)
        probs = jax.nn.softmax(logits, axis=2)
        out = jnp.einsum('bijh,bjhc->bihc', probs, f)
        return out.reshape(B, N, H * c)

    h = jnp.maximum(_layernorm(x, axis=-1), 0.0)
    x = x + _L0_gnn_ref(h, adj, L0_gnn_W, L0_gnn_a_src, L0_gnn_a_dst)
    h = jnp.maximum(_layernorm(x, axis=-1), 0.0)
    x = x + _L1_gnn_ref(h, adj, L1_gnn_W, L1_gnn_b, L1_gnn_a)
    return x


_drawn_inputs = setup_inputs


def setup_inputs(seed=0):
    import zlib

    import numpy as np

    out = dict(_drawn_inputs(seed))
    spreads = {'L1_gnn_b': (0.0, 0.1)}
    factors = {}
    for name, (base, spread) in spreads.items():
        noise = np.random.default_rng([zlib.crc32(name.encode()), seed]).standard_normal(out[name].shape)
        drawn = base * np.exp(spread * noise) if base else spread * noise
        out[name] = jnp.asarray(drawn.astype(out[name].dtype))
    for name, factor in factors.items():
        out[name] = (out[name] * factor).astype(out[name].dtype)
    return out
```

```python
import concourse.bass as bass
from concourse import mybir
from contextlib import ExitStack


def gat_two_layers(nc: bass.Bass, x_in: bass.AP, adj: bass.AP, W0: bass.AP, a0_src: bass.AP, a0_dst: bass.AP,
                   W1: bass.AP, b1: bass.AP, a1: bass.AP, out: bass.AP):
    fp32, bf16, u8 = mybir.dt.float32, mybir.dt.bfloat16, mybir.dt.uint8
    ALU, ACT, AX = mybir.AluOpType, mybir.ActivationFunctionType, mybir.AxisListType

    B, N, F = x_in.shape
    P = 128
    KC = F // P
    NJ = N // P
    CH = 4
    NC = NJ // CH
    CI = CH * P
    H = a1.shape[0]
    C = F // H
    E0 = F + 2
    EH = C + 2
    E1 = H * EH
    HEADS = (1, H)
    COLS = (E0, E1)
    RING = 8
    LEAKY = 0.2
    EPS = 1e-5
    TINY = 1.2e-38
    CHUNKS = B * NC
    MSLOTS = 2 * NC

    def order(do_a, do_b, do_m):
        a_tiles = [("P", 0, 0, j) for j in range(NJ)]
        cuts = [0, 0, 6, 11, 16]
        out_order = []
        for h in range(H):
            if do_a:
                out_order += a_tiles[cuts[h]:cuts[h + 1]] if do_b else a_tiles[4 * h:4 * h + 4]
                if h == H - 1:
                    out_order += [("E", 0, 0)]
            if do_b:
                tiles = [("P", 1, h, j) for j in range(NJ)]
                out_order += tiles[:8]
                if do_m:
                    out_order += [("M", h, 0)]
                if h:
                    out_order += [("R", h - 1)]
                out_order += tiles[8:] + [("E", 1, h)]
            elif do_m:
                out_order += [("M", h, 0)]
            if do_m:
                out_order += [("M", h, 1)]
        if do_b:
            out_order += [("R", H - 1)]
        if do_a:
            out_order += [("R", H)]
        return out_order

    STEP_A, STEP_AB, STEP_ABN, STEP_B = order(1, 0, 1), order(1, 1, 1), order(1, 1, 0), order(0, 1, 0)

    ctx = ExitStack()
    with ctx:
        def sb(name, shape, dt=fp32):
            return ctx.enter_context(nc.sbuf_tensor(name, shape, dt))

        def pb(name, shape, dt=fp32):
            return ctx.enter_context(nc.psum_tensor(name, shape, dt))

        def sem(name):
            return ctx.enter_context(nc.semaphore(name))

        mask = sb("mask", [P, MSLOTS, NJ, CI], u8)
        tiles = sb("tiles", [P, RING, CI])
        xb = sb("xb", [P, MSLOTS, CH, F])
        S0 = sb("S0", [P, NJ, E0])
        S1 = sb("S1", [P, NJ, E1])
        Rb = sb("Rb", [P, H + 1, CI])
        adj_rows = sb("adj_rows", [P, CH, N], bf16)
        y = sb("y", [P, 2, CH, F])
        yT = sb("yT", [P, 2, KC, CI])
        numA = sb("numA", [P, CH, F + 1])
        numB = sb("numB", [P, 2, CH, C + 1])
        WT = [sb("WT0", [P, KC, E0]), sb("WT1", [P, KC, E1])]
        Wn = sb("Wn", [P, 2, KC, F])
        a_cols = sb("a_cols", [P, KC, 2 + 2 * H])
        b_col = sb("b_col", [P, KC])
        bias = sb("bias", [P, E1])
        ident = sb("ident", [P, P])
        identb = sb("identb", [P, P], bf16)
        mean_h = [sb("mean_h0", [P, E0]), sb("mean_h1", [P, E1])]
        ysum = sb("ysum", [P, KC, NC])
        ysums = sb("ysums", [P, KC])
        stats = sb("stats", [P, 2, CH, 6])
        mv = sb("mv", [P, 2, CH, 2])
        var_eps = sb("var_eps", [P, 2, CH])
        neg_mean = sb("neg_mean", [P, 2, CH])
        minus_half = sb("minus_half", [P, CH])
        minus_one = sb("minus_one", [P, CH])
        alone_now = sb("alone_now", [P, CH])
        rstd = sb("rstd", [P, 2, CH])
        shift = sb("shift", [P, 2, CH])
        d_part = sb("d_part", [P, H])
        d_max = [sb("d_max0", [P, 1]), sb("d_max1", [P, H])]
        dd = [sb("dd0", [P, NJ, 1]), sb("dd1", [P, NJ, H])]
        ss = [sb("ss0", [P, NJ, 1]), sb("ss1", [P, NJ, H])]
        w = [sb("w0", [P, NJ, 1]), sb("w1", [P, NJ, H])]
        v = [sb("v0", [P, NJ, 1]), sb("v1", [P, NJ, H])]
        R = sb("R", [P, NJ, H + 1])
        R_now = sb("R_now", [P, CH, H + 1])
        alone = sb("alone", [P, NC, CH])
        denA = sb("denA", [P, CH])
        denB = sb("denB", [P, CH])

        accA = pb("accA", [P, CH, 512])
        accB = pb("accB", [P, 2, 512])
        turn_ps = pb("turn_ps", [P, 8, P], bf16)
        misc_ps = pb("misc_ps", [P, 512])

        names = """w_loaded consts prep_t prep_e x_loaded0 x_loaded1 x_loaded2 x_loaded3 adj0 adj1 adj2 adj3
            stats_done mv_ready ve_ready rstd_ready norm_ready y_ready yt_turned yt_ready feat_done feat_moved
            chain exp_ready hv_ready misc_done misc_used tile_ready tile_free mask_turned mask_ready
            a_moved a_den a_quot x1_ready x1_full b_moved b_den b_quot x2_ready out_done r_now passed""".split()
        S = {n: sem(n) for n in names}
        x_loaded = [S[f"x_loaded{t}"] for t in range(NC)]
        adj_loaded = [S[f"adj{r}"] for r in range(CH)]

        def heads_view(t, col, n):
            if t is S0:
                return S0[:, :, F + col:F + col + 1]
            return S1[:, :, :].rearrange("p j (h e) -> p j h e", h=H)[:, :, :, C + col]

        def layer_index(ph, L):
            return 2 * ph if L == 0 else 2 * ph - 1

        def tiles_before(kind, ph, c):
            if kind == "A":
                return NJ * c
            full = NJ * (1 + H)
            if kind == "B":
                return NJ * NC + full * NC * (B - 1) + NJ * H * c
            return full * NC * ph + (full * c - full * NC + NJ * NC)

        def misc_before(kind, ph):
            first = 3 + NC
            each = 3 + (2 + H) + (H + 1) * NC
            return 0 if kind == "A" else each * ph + (first - each)

        def misc_before_layer(kind, ph, L):
            return misc_before(kind, ph) + (2 + H if L == 0 and kind != "A" else 0)

        def misc_before_step(kind, ph, c):
            if kind == "A":
                return 3 + c
            if kind == "B":
                return misc_before(kind, ph) + (2 + H) + H * c
            return misc_before(kind, ph) + (5 + H) + (H + 1) * c

        def r_now_before(kind, ph):
            return 0 if kind == "A" else (NC + 2) * ph + (NC + 1 - (NC + 2))

        def rb_for(kind, ph, c, unit):
            if kind == "A":
                return 3 + c
            if kind == "B":
                return misc_before(kind, ph) + H * c + (3 + unit)
            return misc_before(kind, ph) + (H + 1) * c + (5 + unit)

        def last_tiles(events):
            found, i = {}, 0
            for e in events:
                if e[0] == "P":
                    i += 1
                    found[H if e[1] == 0 else e[2]] = i
            return found

        def wait(eng, s, value):
            if not isinstance(value, int) or value > 0:
                eng.wait_ge(s, value)

        def wait_alone(eng, s, value):
            wait(eng, s, value)
            eng.sem_inc(S["passed"], 1)

        def phases(eng, layer, steps, before_last=None):
            layer("A", 0, 0)
            with eng.Fori(0, NC) as c:
                steps("A", STEP_A, 0, c)
            with eng.Fori(1, B - 1) as ph:
                layer("AB", ph, 1)
                layer("AB", ph, 0)
                with eng.Fori(0, NC) as c:
                    steps("AB", STEP_AB, ph, c)
            layer("AB", B - 1, 1)
            layer("AB", B - 1, 0)
            if before_last:
                before_last()
            with eng.Fori(0, NC) as c:
                steps("AB", STEP_ABN, B - 1, c)
            layer("B", B, 1)
            with eng.Fori(0, NC) as c:
                steps("B", STEP_B, B, c)

        block = ctx.enter_context(nc.Block())

        @block.sync
        def _(sp):
            def load_x(m, t):
                return sp.dma_start(xb[:, m % MSLOTS, :, :],
                                    x_rows[m, :, :, :]).then_inc(x_loaded[t], 16)

            x_rows = x_in.rearrange("b (c k p) f -> (b c) p k f", k=CH, p=P)
            out_rows = out.rearrange("b (c k p) f -> (b c) p k f", k=CH, p=P)
            for L, Wd in enumerate((W0, W1)):
                sp.dma_start(Wn[:, L, :, :], Wd.rearrange("(k p) f -> p k f", p=P)).then_inc(S["w_loaded"], 16)
            sp.wait_ge(S["consts"], 1)
            with nc.allow_non_contiguous_dma("small vectors, once"):
                for col, a in enumerate((a0_dst, a0_src)):
                    sp.dma_start(a_cols[:, :, col], a.rearrange("(k p) -> p k", p=P)).then_inc(S["w_loaded"], 16)
                sp.dma_start(b_col[:, :], b1.rearrange("(k p) -> p k", p=P)).then_inc(S["w_loaded"], 16)
                for h in range(H):
                    p0, k = h * C % P, h * C // P
                    for which in range(2):
                        sp.dma_start(a_cols[p0:p0 + C, k, 2 + 2 * h + which],
                                     a1[h, (1 - which) * C:(2 - which) * C]).then_inc(S["w_loaded"], 16)
            sp.dma_start(bias[:, :].rearrange("p (h e) -> p h e", h=H)[:, :, 0:C],
                         b1.rearrange("(h c) -> h c", h=H).partition_broadcast(P)).then_inc(S["w_loaded"], 16)
            for m in range(MSLOTS):
                if m >= NC:
                    sp.wait_ge(x_loaded[m - NC], 16)
                load_x(m, m % NC)

            def store(m):
                sp.wait_ge(S["x2_ready"], H * m + (H + 2))
                sp.dma_start(out_rows[m, :, :, :], xb[:, m % MSLOTS, :, :]).then_inc(S["out_done"], 16)
                wait_alone(sp, S["out_done"], 16 * m + 16)

            with sp.Fori(0, B - 2) as b:
                for t in range(NC):
                    store(NC * b + t)
                    load_x(NC * b + (t + MSLOTS), t)
            with sp.Fori(NC * (B - 2), CHUNKS) as m:
                store(m)

        @block.gpsimd
        def _(pool):
            adj_view = adj.rearrange("b (q r p) n -> (b q) r p n", r=CH, p=P)

            def load_adj(q, r):
                wait(pool, S["mask_turned"], 2 * CH * (q - 1) + (2 * r + 2))
                pool.dma_start(adj_rows[:, r, :], adj_view[q, r, :, :]).then_inc(adj_loaded[r], 16)

            pool.sem_inc(S["x1_ready"], 1)
            pool.sem_inc(S["x2_ready"], 2)
            pool.memset(a_cols[:, :, :], 0.0).then_inc(S["consts"], 1)
            for r in range(CH):
                load_adj(0, r)
            pool.memset(minus_half[:, :], -0.5)
            pool.memset(minus_one[:, :], -1.0)
            pool.memset(R[:, :, :], 0.0)
            for t in (ident, identb):
                last = pool.memset(t[:, :], 0.0)
            last.then_inc(S["consts"], 1)
            pool.wait_ge(S["consts"], 2)
            for t in (ident, identb):
                last = pool.affine_select(out=t[:, :], in_=t[:, :], compare_op=ALU.not_equal, fill=1.0, base=0,
                                          pattern=[[-1, P]], channel_multiplier=1)
            last.then_inc(S["consts"], 1)
            for q in range(1, NC):
                for r in range(CH):
                    load_adj(q, r)

            def layer(kind, ph, L):
                first = NC * layer_index(ph, L)
                for t in range(NC):
                    f, s = first + t, t % 2
                    pool.wait_ge(S["mv_ready"], f + 1)
                    wait_alone(pool, S["y_ready"], CH * (f - 1))
                    pool.tensor_scalar(var_eps[:, s, :], mv[:, s, :, 1], EPS, None, ALU.add)
                    pool.tensor_scalar(neg_mean[:, s, :], mv[:, s, :, 0], -1.0, None, ALU.mult)\
                        .then_inc(S["ve_ready"], 1)
                    pool.wait_ge(S["ve_ready"], f + 1)
                    pool.tensor_tensor(rstd[:, s, :], var_eps[:, s, :], minus_half[:, :], ALU.pow)\
                        .then_inc(S["rstd_ready"], 1)
                    pool.wait_ge(S["rstd_ready"], f + 1)
                    pool.tensor_tensor(shift[:, s, :], rstd[:, s, :], neg_mean[:, s, :], ALU.mult)\
                        .then_inc(S["norm_ready"], 1)

            def steps(kind, events, ph, c):
                n = ph * NC + c
                for e in events:
                    if e[0] == "E" and e[1] == 0:
                        xs = xb[:, n % MSLOTS, :, :]
                        wait_alone(pool, S["a_moved"], n + 2)
                        pool.tensor_scalar(alone_now[:, :], numA[:, :, F], 0.0, None, ALU.is_equal)
                        pool.tensor_scalar(denA[:, :], numA[:, :, F], TINY, None, ALU.max).then_inc(S["a_den"], 1)
                        pool.wait_ge(S["a_den"], 2 * n + 1)
                        pool.tensor_copy(alone[:, c, :], alone_now[:, :])
                        pool.tensor_tensor(denA[:, :], denA[:, :], minus_one[:, :], ALU.pow)\
                            .then_inc(S["a_den"], 1)
                        pool.wait_ge(S["a_den"], 2 * n + 2)
                        pool.tensor_tensor(numA[:, :, 0:F], numA[:, :, 0:F],
                                           denA[:, :].unsqueeze(2).to_broadcast([P, CH, F]), ALU.mult)\
                            .then_inc(S["a_quot"], 1)
                        pool.wait_ge(S["a_quot"], n + 1)
                        pool.tensor_tensor(xs, xs, numA[:, :, 0:F], ALU.add).then_inc(S["x1_ready"], 1)
                    elif e[0] == "E":
                        h, s = e[2], e[2] % 2
                        g = H * (n - NC) + h
                        xs = xb[:, (n + NC) % MSLOTS, :, h * C:(h + 1) * C]
                        wait_alone(pool, S["b_moved"], g + 3)
                        pool.tensor_scalar(denB[:, :], numB[:, s, :, C], TINY, None, ALU.max)\
                            .then_inc(S["b_den"], 1)
                        pool.wait_ge(S["b_den"], 2 * g + 1)
                        pool.tensor_tensor(denB[:, :], denB[:, :], minus_one[:, :], ALU.pow)\
                            .then_inc(S["b_den"], 1)
                        pool.wait_ge(S["b_den"], 2 * g + 2)
                        pool.tensor_tensor(numB[:, s, :, 0:C], numB[:, s, :, 0:C],
                                           denB[:, :].unsqueeze(2).to_broadcast([P, CH, C]), ALU.mult)\
                            .then_inc(S["b_quot"], 1)
                        pool.wait_ge(S["b_quot"], g + 1)
                        pool.tensor_tensor(xs, xs, numB[:, s, :, 0:C], ALU.add).then_inc(S["x2_ready"], 1)
                    elif e[0] == "M" and e[2] == 1 and kind != "B":
                        load_adj(n + NC, e[1])

            phases(pool, layer, steps)

        @block.scalar
        def _(act):
            act.sem_inc(S["a_moved"], 1)
            act.sem_inc(S["b_moved"], 2)
            for L in range(2):
                for k in range(KC):
                    i = 2 * (KC * L + k)
                    act.wait_ge(S["prep_t"], i + 1)
                    src = accA[:, 0, 0:F]
                    if L == 0:
                        nc.scalar.activation(WT[0][:, k, 0:F], src, ACT.Copy).then_inc(S["prep_e"], 1)
                    else:
                        nc.scalar.activation(WT[1][:, k, :].rearrange("p (h e) -> p h e", h=H)[:, :, 0:C],
                                             src.rearrange("p (h c) -> p h c", h=H), ACT.Copy)\
                            .then_inc(S["prep_e"], 1)
                    act.wait_ge(S["prep_t"], i + 2)
                    if L == 0:
                        nc.scalar.activation(WT[0][:, k, F:F + 2], accA[:, 1, 0:2], ACT.Copy)\
                            .then_inc(S["prep_e"], 1)
                    else:
                        nc.scalar.activation(WT[1][:, k, :].rearrange("p (h e) -> p h e", h=H)[:, :, C:C + 2],
                                             accA[:, 1, 0:2 * H].rearrange("p (h e) -> p h e", h=H), ACT.Copy)\
                            .then_inc(S["prep_e"], 1)
            act.wait_ge(S["prep_t"], 4 * KC + 1)
            nc.scalar.activation(bias[:, :].rearrange("p (h e) -> p h e", h=H)[:, :, C:C + 2],
                                 accA[:, 2, 0:2 * H].rearrange("p (h e) -> p h e", h=H), ACT.Copy)\
                .then_inc(S["prep_e"], 1)

            def move_mask(q, r, half):
                g = 2 * CH * q + (2 * r + half)
                act.wait_ge(S["mask_turned"], g + 1)
                nc.scalar.activation(mask[:, q % MSLOTS, 8 * half:8 * half + 8, r * P:(r + 1) * P],
                                     turn_ps[:, :, :], ACT.Copy).then_inc(S["mask_ready"], 1)

            def move_rb(misc, unit):
                act.wait_ge(S["misc_done"], misc + 1)
                nc.scalar.activation(Rb[:, unit, :], misc_ps[:, :], ACT.Copy).then_inc(S["misc_used"], 1)

            for q in range(NC - 1):
                for r in range(CH):
                    for half in range(2):
                        move_mask(q, r, half)

            def layer(kind, ph, L):
                first = NC * layer_index(ph, L)
                b = ph - L
                for t in range(NC):
                    f, s = first + t, t % 2
                    act.wait_ge(S["norm_ready"], f + 1)
                    wait(act, S["yt_turned"], f - 1)
                    for k in range(CH):
                        nc.scalar.activation(y[:, s, k, :], xb[:, (NC * b + t) % MSLOTS, k, :], ACT.Relu,
                                             bias=shift[:, s, k:k + 1], scale=rstd[:, s, k:k + 1])\
                            .then_inc(S["y_ready"], 1)
                    act.wait_ge(S["yt_turned"], f + 1)
                    wait(act, S["feat_done"], CH * (f - 1))
                    for k in range(KC):
                        nc.scalar.activation(yT[:, s, k, :], accA[:, k, :], ACT.Copy,
                                             accum_out=ysum[:, k, t:t + 1]).then_inc(S["yt_ready"], 1)
                i = layer_index(ph, L)
                act.wait_ge(S["chain"], 4 * i + 4)
                nc.scalar.activation(w[L][:, :, :], dd[L][:, :, :], ACT.Exp, scale=1 - LEAKY)
                nc.scalar.activation(v[L][:, :, :], dd[L][:, :, :], ACT.Exp, scale=LEAKY)\
                    .then_inc(S["exp_ready"], 1)
                col = slice(H, H + 1) if L == 0 else slice(0, H)
                nc.scalar.activation(R[:, :, col], ss[L][:, :, :], ACT.Exp, scale=-(1 - LEAKY))\
                    .then_inc(S["exp_ready"], 1)
                act.wait_ge(S["exp_ready"], 2 * i + 2)
                nc.scalar.activation(R_now[:, :, col], R[:, 0:CH, col], ACT.Copy).then_inc(S["r_now"], 1)
                m = misc_before_layer(kind, ph, L) + 2
                for unit in ([H] if L == 0 else range(H)):
                    move_rb(m, unit)
                    m = m + 1

            def steps(kind, events, ph, c):
                n = ph * NC + c
                misc = misc_before_step(kind, ph, c)
                last_tile = last_tiles(events)
                first_r = True
                for e in events:
                    if e[0] == "M":
                        move_mask(n + (NC - 1), e[1], e[2])
                    elif e[0] == "R":
                        if first_r:
                            nc.scalar.activation(R_now[:, :, :],
                                                 R[:, :, :].rearrange("p (c k) u -> p c k u", k=CH)[:, (c + 1) % NC, :, :],
                                                 ACT.Copy).then_inc(S["r_now"], 1)
                            first_r = False
                        act.wait_ge(S["tile_ready"], tiles_before(kind, ph, c) + last_tile[e[1]])
                        move_rb(misc, e[1])
                        misc = misc + 1
                    elif e[0] == "E" and e[1] == 0:
                        act.wait_ge(S["tile_free"], tiles_before(kind, ph, c) + (RING + last_tile[H]))
                        act.wait_ge(S["x1_ready"], n + 1)
                        nc.scalar.activation(numA[:, :, :], accA[:, :, 0:F + 1], ACT.Copy)\
                            .then_inc(S["a_moved"], 1)
                    elif e[0] == "E":
                        h = e[2]
                        g = H * (n - NC) + h
                        act.wait_ge(S["tile_free"], tiles_before(kind, ph, c) + (RING + last_tile[h]))
                        act.wait_ge(S["x2_ready"], g + 1)
                        nc.scalar.activation(numB[:, h % 2, :, :],
                                             accB[:, h % 2, 0:CH * (C + 1)].rearrange("p (k e) -> p k e", k=CH),
                                             ACT.Copy).then_inc(S["b_moved"], 1)

            def before_last():
                for r in range(CH):
                    for half in range(2):
                        move_mask(CHUNKS - 1, r, half)

            phases(act, layer, steps, before_last)

        @block.tensor
        def _(pe):
            pe.wait_ge(S["consts"], 3)
            pe.wait_ge(S["w_loaded"], 16 * (6 + 2 * H))
            for L in range(2):
                acols = a_cols[:, :, 0:2] if L == 0 else a_cols[:, :, 2:2 + 2 * H]
                na = 2 * HEADS[L]
                for k in range(KC):
                    i = 2 * (KC * L + k)
                    wait(pe, S["prep_e"], i)
                    for o in range(KC):
                        last = nc.tensor.transpose(accA[:, 0, o * P:(o + 1) * P],
                                                   Wn[:, L, o, k * P:(k + 1) * P], ident[:, :])
                    last.then_inc(S["prep_t"], 1)
                    for o in range(KC):
                        last = nc.tensor.matmul(accA[:, 1, 0:na], Wn[:, L, o, k * P:(k + 1) * P],
                                                acols[:, o, :], start=o == 0, stop=o == KC - 1)
                    last.then_inc(S["prep_t"], 1)
            for o in range(KC):
                last = nc.tensor.matmul(accA[:, 2, 0:2 * H], b_col[:, o:o + 1].to_broadcast([P, P]),
                                        a_cols[:, o, 2:2 + 2 * H], start=o == 0, stop=o == KC - 1)
            last.then_inc(S["prep_t"], 1)
            pe.wait_ge(S["prep_e"], 4 * KC + 1)

            def turn_mask(q, r, half):
                g = 2 * CH * q + (2 * r + half)
                if half == 0:
                    pe.wait_ge(adj_loaded[r], 16 * q + 16)
                wait(pe, S["mask_ready"], g)
                for j in range(8):
                    col = (8 * half + j) * P
                    last = nc.tensor.transpose(turn_ps[:, j, :], adj_rows[:, r, col:col + P], identb[:, :])
                last.then_inc(S["mask_turned"], 1)

            def turn_r(misc, unit):
                wait(pe, S["misc_used"], misc)
                for k in range(CH):
                    last = nc.tensor.transpose(misc_ps[:, k * P:(k + 1) * P],
                                               R_now[:, k, unit:unit + 1].to_broadcast([P, P]), ident[:, :])
                last.then_inc(S["misc_done"], 1)

            for q in range(NC - 1):
                for r in range(CH):
                    for half in range(2):
                        turn_mask(q, r, half)

            def layer(kind, ph, L):
                i = layer_index(ph, L)
                first = NC * i

                def turn_y(t):
                    f, s = first + t, t % 2
                    wait(pe, S["yt_ready"], 2 * f)
                    for k in range(CH):
                        pe.wait_ge(S["y_ready"], CH * f + (k + 1))
                        for kc in range(KC):
                            last = nc.tensor.transpose(accA[:, kc, k * P:(k + 1) * P],
                                                       y[:, s, k, kc * P:(kc + 1) * P], ident[:, :])
                    last.then_inc(S["yt_turned"], 1)

                if L == 1:
                    pe.wait_ge(S["a_moved"], ph * NC + 1)
                turn_y(0)
                for t in range(NC):
                    if t + 1 < NC:
                        turn_y(t + 1)
                    f, s = first + t, t % 2
                    pe.wait_ge(S["yt_ready"], 2 * f + 2)
                    for k in range(CH):
                        g = CH * f + k
                        wait(pe, S["feat_moved"], g - 1)
                        for kc in range(KC):
                            last = nc.tensor.matmul(accA[:, 2 + k % 2, 0:COLS[L]], yT[:, s, kc, k * P:(k + 1) * P],
                                                    WT[L][:, kc, :], start=kc == 0, stop=kc == KC - 1)
                        last.then_inc(S["feat_done"], 1)
                m = misc_before_layer(kind, ph, L)
                pe.wait_ge(S["chain"], 4 * i + 1)
                wait(pe, S["misc_used"], m)
                for h in range(HEADS[L]):
                    last = nc.tensor.transpose(misc_ps[:, h * P:(h + 1) * P], d_part[:, h:h + 1].to_broadcast([P, P]),
                                               ident[:, :])
                last.then_inc(S["misc_done"], 1)
                pe.wait_ge(S["chain"], 4 * i + 2)
                pe.wait_ge(S["misc_used"], m + 1)
                for kc in range(KC):
                    last = nc.tensor.matmul(misc_ps[:, 0:COLS[L]], ysums[:, kc:kc + 1].to_broadcast([P, P]),
                                            WT[L][:, kc, :], start=kc == 0, stop=kc == KC - 1)
                last.then_inc(S["misc_done"], 1)
                pe.wait_ge(S["r_now"], r_now_before(kind, ph) + (1 if L == 1 or kind == "A" else 2))
                m = m + 2
                for unit in ([H] if L == 0 else range(H)):
                    turn_r(m, unit)
                    m = m + 1
                wait_alone(pe, S["hv_ready"], first + NC)

            def steps(kind, events, ph, c):
                n = ph * NC + c
                first_tile = tiles_before(kind, ph, c)
                misc = misc_before_step(kind, ph, c)
                i = 0
                first_r = True
                for e in events:
                    if e[0] == "P":
                        L, h, j = e[1:]
                        slot = i % RING
                        if L == 0 and j == 0:
                            pe.wait_ge(S["a_moved"], n + 1)
                        if L == 1 and j == 0:
                            pe.wait_ge(S["b_moved"], H * (n - NC) + (h + 1))
                        pe.wait_ge(S["tile_ready"], first_tile + (i + 1))
                        for k in range(CH):
                            lhsT = tiles[:, slot, k * P:(k + 1) * P]
                            if L == 0:
                                last = nc.tensor.matmul(accA[:, k, 0:F + 1], lhsT, S0[:, j, 0:F + 1],
                                                        start=j == 0, stop=j == NJ - 1)
                            else:
                                last = nc.tensor.matmul(accB[:, h % 2, k * (C + 1):(k + 1) * (C + 1)], lhsT,
                                                        S1[:, j, h * EH:h * EH + C + 1],
                                                        start=j == 0 and k == 0, stop=j == NJ - 1,
                                                        skip_group_check=True)
                        last.then_inc(S["tile_free"], 1)
                        i += 1
                    elif e[0] == "M":
                        turn_mask(n + (NC - 1), e[1], e[2])
                    elif e[0] == "R":
                        if first_r:
                            pe.wait_ge(S["r_now"], r_now_before(kind, ph) + c + (3 if kind == "AB" else 2))
                            first_r = False
                        turn_r(misc, e[1])
                        misc = misc + 1

            def before_last():
                for r in range(CH):
                    for half in range(2):
                        turn_mask(CHUNKS - 1, r, half)

            phases(pe, layer, steps, before_last)

        @block.vector
        def _(dve):
            dve.sem_inc(S["tile_free"], RING)

            def layer(kind, ph, L):
                i = layer_index(ph, L)
                first = NC * i
                b = ph - L
                if L == 1:
                    dve.wait_ge(S["x1_ready"], NC * ph + 1)
                for t in range(NC):
                    f, s = first + t, t % 2
                    m = NC * b + t
                    xs = xb[:, m % MSLOTS, :, :]
                    if L == 0:
                        dve.wait_ge(x_loaded[t], 16 * b + 16)
                    else:
                        for k in range(CH):
                            last = nc.vector.scalar_tensor_tensor(
                                out=xs[:, k, :], in0=mean_h[0][:, 0:F], scalar=alone[:, t, k:k + 1],
                                in1=xs[:, k, :], op0=ALU.mult, op1=ALU.add)
                        last.then_inc(S["x1_full"], 1)
                        dve.wait_ge(S["x1_full"], NC * b + (t + 1))
                    wait_alone(dve, S["norm_ready"], f - 1)
                    for k in range(CH):
                        last = nc.vector.bn_stats(stats[:, s, k, :], xs[:, k, :])
                    last.then_inc(S["stats_done"], 1)
                    wait_alone(dve, S["stats_done"], f + 1)
                    for k in range(CH):
                        last = nc.vector.bn_aggr(mv[:, s, k, :], stats[:, s, k, :])
                    last.then_inc(S["mv_ready"], 1)
                for t in range(NC):
                    for k in range(CH):
                        g = CH * (first + t) + k
                        j = CH * t + k
                        dve.wait_ge(S["feat_done"], g + 1)
                        src = accA[:, 2 + k % 2, 0:COLS[L]]
                        if L == 0:
                            nc.vector.tensor_copy(S0[:, j, :], src).then_inc(S["feat_moved"], 1)
                        else:
                            nc.vector.tensor_tensor(S1[:, j, :], src, bias[:, :], ALU.add)\
                                .then_inc(S["feat_moved"], 1)
                nh = HEADS[L]
                SL = (S0, S1)[L]
                d, s_ = heads_view(SL, 0, nh), heads_view(SL, 1, nh)
                m = misc_before_layer(kind, ph, L)
                dve.wait_ge(S["feat_moved"], CH * (first + NC))
                nc.vector.tensor_reduce(d_part[:, 0:nh], d.rearrange("p j h -> p h j"), AX.X, ALU.max)\
                    .then_inc(S["chain"], 1)
                dve.wait_ge(S["yt_ready"], 2 * (first + NC))
                nc.vector.tensor_reduce(ysums[:, :], ysum[:, :, :], AX.X, ALU.add).then_inc(S["chain"], 1)
                dve.wait_ge(S["misc_done"], m + 1)
                nc.vector.tensor_reduce(d_max[L][:, :], misc_ps[:, 0:nh * P].rearrange("p (h n) -> p h n", h=nh),
                                        AX.X, ALU.max).then_inc(S["misc_used"], 1)
                dve.wait_ge(S["misc_used"], m + 1)
                dmax_b = d_max[L][:, :].unsqueeze(1).to_broadcast([P, NJ, nh])
                nc.vector.tensor_tensor(dd[L][:, :, :], d, dmax_b, ALU.subtract)
                nc.vector.tensor_tensor(ss[L][:, :, :], s_, dmax_b, ALU.add).then_inc(S["chain"], 1)
                dve.wait_ge(S["chain"], 4 * i + 3)
                nc.vector.tensor_scalar(ss[L][:, :, :], ss[L][:, :, :], 0.0, None, ALU.max)\
                    .then_inc(S["chain"], 1)
                dve.wait_ge(S["misc_done"], m + 2)
                if L == 0:
                    nc.vector.tensor_scalar(mean_h[0][:, :], misc_ps[:, 0:E0], 1.0 / N, None, ALU.mult)\
                        .then_inc(S["misc_used"], 1)
                else:
                    nc.vector.scalar_tensor_tensor(out=mean_h[1][:, :], in0=misc_ps[:, 0:E1], scalar=1.0 / N,
                                                   in1=bias[:, :], op0=ALU.mult, op1=ALU.add)\
                        .then_inc(S["misc_used"], 1)
                dve.wait_ge(S["exp_ready"], 2 * i + 1)
                for t in range(NC):
                    js = slice(CH * t, CH * t + CH)
                    if L == 0:
                        for j in range(CH * t, CH * t + CH):
                            nc.vector.tensor_scalar(S0[:, j, 0:F], S0[:, j, 0:F], v[0][:, j, :], None, ALU.mult)
                        nc.vector.tensor_copy(S0[:, js, F:F + 1], v[0][:, js, :]).then_inc(S["hv_ready"], 1)
                    else:
                        part = S1[:, js, :].rearrange("p j (h e) -> p (j h) e", h=H)
                        vs = v[1][:, js, :].rearrange("p j h -> p (j h)").unsqueeze(2)
                        nc.vector.tensor_tensor(part[:, :, 0:C], part[:, :, 0:C],
                                                vs.to_broadcast([P, CH * H, C]), ALU.mult)
                        nc.vector.tensor_copy(part[:, :, C:C + 1], vs).then_inc(S["hv_ready"], 1)
                if L == 1:
                    dve.wait_ge(S["misc_used"], m + 2)
                    dve.wait_ge(S["y_ready"], CH * (first + NC))
                    for t in range(NC):
                        for k in range(CH):
                            xk = xb[:, (NC * b + t) % MSLOTS, k, :].rearrange("p (h c) -> p h c", h=H)
                            nc.vector.scalar_tensor_tensor(
                                out=xk, in0=mean_h[1][:, :].rearrange("p (h e) -> p h e", h=H)[:, :, 0:C],
                                scalar=alone[:, t, k:k + 1], in1=xk, op0=ALU.mult, op1=ALU.add)

            def steps(kind, events, ph, c):
                n = ph * NC + c
                first_tile = tiles_before(kind, ph, c)
                i = 0
                for e in events:
                    if e[0] != "P":
                        continue
                    L, h, j = e[1:]
                    unit = H if L == 0 else h
                    slot = i % RING
                    if j == 0:
                        dve.wait_ge(S["misc_used"], rb_for(kind, ph, c, unit if kind != "A" else 0))
                    if L == 0 and j == 0:
                        dve.wait_ge(S["mask_ready"], 2 * CH * n + 2 * CH)
                    if i % 2 == 0:
                        dve.wait_ge(S["tile_free"], first_tile + (i + 2))
                    ms = mask[:, (n if L == 0 else n + NC) % MSLOTS, j, :]
                    nc.vector.scalar_tensor_tensor(out=tiles[:, slot, :], in0=Rb[:, unit, :], scalar=w[L][:, j, h:h + 1],
                                                   in1=ms, op0=ALU.max, op1=ALU.mult).then_inc(S["tile_ready"], 1)
                    i += 1

            phases(dve, layer, steps)


def kernel(x, adj, L0_gnn_W, L0_gnn_a_src, L0_gnn_a_dst, L1_gnn_W, L1_gnn_b, L1_gnn_a):
    import numpy as np
    import concourse.bacc as bacc
    from concourse.bass_utils import run_bass_kernel_spmd

    nc = bacc.Bacc("TRN2", target_bir_lowering=False, num_devices=1)
    given = dict(x=x, adj=adj, W0=L0_gnn_W, a0_src=L0_gnn_a_src, a0_dst=L0_gnn_a_dst,
                 W1=L1_gnn_W, b1=L1_gnn_b, a1=L1_gnn_a)
    arrays = {f"in_{name}": np.ascontiguousarray(a) for name, a in given.items()}
    args = [nc.dram_tensor(name, a.shape, mybir.dt.from_np(a.dtype), kind="ExternalInput").ap()
            for name, a in arrays.items()]
    out = nc.dram_tensor("out", arrays["in_x"].shape, mybir.dt.float32, kind="ExternalOutput").ap()
    gat_two_layers(nc, *args, out)
    return run_bass_kernel_spmd(nc, [arrays], core_ids=[0]).results[0]["out"]
```

```python
import concourse.bass as bass
from concourse import mybir
from contextlib import ExitStack


def gat_two_layers(nc: bass.Bass, x_in: bass.AP, adj: bass.AP, W0: bass.AP, a0_src: bass.AP, a0_dst: bass.AP,
                   W1: bass.AP, b1: bass.AP, a1: bass.AP, out: bass.AP):
    fp32, bf16, fp16 = mybir.dt.float32, mybir.dt.bfloat16, mybir.dt.float16
    u8, i8, u32, fp8 = mybir.dt.uint8, mybir.dt.int8, mybir.dt.uint32, mybir.dt.float8e4
    ALU, ACT, AX = mybir.AluOpType, mybir.ActivationFunctionType, mybir.AxisListType

    B, N, F = x_in.shape
    P = 128
    KC = F // P
    NJ = N // P
    CH = 4
    NC = NJ // CH
    CI = CH * P
    H = a1.shape[0]
    C = F // H
    E0 = F + 2
    EH = C + 2
    E1 = H * EH
    HEADS = (1, H)
    COLS = (E0, E1)
    RING = 4
    JG = 4
    G = NJ // JG
    HG = H * G
    BRING = 4
    CRING = 2
    CG = HG - G
    LEAD = 3
    CF = C + 1
    NS, NN = 3 * CF, 2 * CF
    ROWS = 2
    MARK = 64.0
    LOW = 2.0 ** 11
    LEAKY = 0.2
    EPS = 1e-5
    TINY = 1.2e-38
    CHUNKS = B * NC
    XSLOTS = 2 * NC
    MSLOTS = NC + 2


    def order(do_a, do_b, do_m, do_l):
        events = []
        for h in range(H):
            last = h == H - 1
            a = [("A", G * h + i) for i in range(G)] if do_a else [None] * G
            g = [("G", h, i) for i in range(G)] if do_b else [None] * G
            m = [("M", h, i) for i in range(2)] if do_m else [None] * 2
            load = [("L", 1 + (h + ROWS) // CH, (h + ROWS) % CH)] if (do_m if h + ROWS < CH else do_l) else []
            r = [("R", h)] if do_b else []
            ra = [("R", H)] if do_a and last else []
            ea = [("EA",)] if do_a and last else []
            eb = [("EB", h)] if do_b else []
            if not last:
                events += [a[0], a[1], g[0], m[0], g[1], a[2], m[1]] + load + [g[2], a[3]] + r + [g[3]] + eb
            else:
                events += [a[0], a[1], m[0], g[0], a[2], m[1]] + load + [g[1], a[3]] + ea + r + [g[2]] + ra + [g[3]] + eb
        return [e for e in events if e]

    def vector_order(events):
        work = [e for e in events if e[0] in "AG"]
        out_order = []
        for i, e in enumerate(work):
            nxt = work[i + 1] if i + 1 < len(work) else None
            if e[0] == "A":
                if nxt and nxt[0] == "G":
                    out_order += [("C0", nxt[2])] if nxt[1] == 0 else []
                    out_order += [("N", nxt[1], nxt[2]), e, ("S", nxt[1], nxt[2])]
                else:
                    out_order += [e]
            elif ("N", e[1], e[2]) not in out_order:
                out_order += [("C0", e[2])] if e[1] == 0 else []
                out_order += [("N", e[1], e[2]), ("S", e[1], e[2])]
        return out_order

    STEP_A, STEP_AB, STEP_B = order(1, 0, 1, 1), order(1, 1, 1, 1), order(0, 1, 0, 0)
    STEP_AB_NEXT_LAST, STEP_AB_LAST = order(1, 1, 1, 0), order(1, 1, 0, 0)
    NR = CRING

    ctx = ExitStack()
    with ctx:
        def sb(name, shape, dt=fp32):
            return ctx.enter_context(nc.sbuf_tensor(name, shape, dt))

        def pb(name, shape, dt=fp32):
            return ctx.enter_context(nc.psum_tensor(name, shape, dt))

        def sem(name):
            return ctx.enter_context(nc.semaphore(name))

        AT_C0 = BRING * 2 * JG * CI
        AT_TILES = AT_C0 + JG * CI
        AT_C = AT_TILES + RING * CI * 4
        AT_NUMA = AT_C + CRING * JG * CI
        AT_NUMS = AT_NUMA + CH * (F + 1) * 4
        AT_NUMN = AT_NUMS + CH * NS * 4
        shared = sb("shared", [P, AT_NUMN + CH * NN * 4], u8)

        def part(at, size, dt):
            return shared[:, at:at + size].bitcast(dt)

        bits = part(0, AT_C0, fp8).rearrange("p (r t j i) -> p r t j i", r=BRING, t=2, j=JG)
        c0 = part(AT_C0, JG * CI, u8).rearrange("p (j i) -> p j i", j=JG)
        tiles = part(AT_TILES, RING * CI * 4, fp32).rearrange("p (r i) -> p r i", r=RING)
        cmp = part(AT_C, CRING * JG * CI, i8).rearrange("p (r j i) -> p r j i", r=CRING, j=JG)
        numA = part(AT_NUMA, CH * (F + 1) * 4, fp32).rearrange("p (k e) -> p k e", k=CH)
        numS = part(AT_NUMS, CH * NS * 4, fp32).rearrange("p (k e) -> p k e", k=CH)
        numN = part(AT_NUMN, CH * NN * 4, fp32).rearrange("p (k e) -> p k e", k=CH)
        S1 = part(0, NJ * E1 * 4, fp32).rearrange("p (j e) -> p j e", j=NJ)
        yT = part(AT_TILES, 2 * KC * CI * 4, fp32).rearrange("p (s k i) -> p s k i", s=2, k=KC)
        y = part(AT_C, 2 * CH * F * 4, fp32).rearrange("p (s k f) -> p s k f", s=2, k=CH)
        Wn = part(AT_TILES, 2 * KC * F * 4, fp32).rearrange("p (l k f) -> p l k f", l=2, k=KC)
        split = part(AT_NUMS, CH * H * CF * 4, fp32).rearrange("p (j e) -> p j e", e=CF)
        squares = part(AT_NUMS, KC * F * 4, fp32).rearrange("p (k f) -> p k f", k=KC)
        assert AT_C + 2 * CH * F * 4 <= AT_NUMS and NJ * E1 * 4 <= AT_TILES

        mask = sb("mask", [P, MSLOTS, NJ, CI], u8)
        xb = sb("xb", [P, XSLOTS, CH, F])
        S0 = sb("S0", [P, NJ, E0])
        Sw = sb("Sw", [P, NJ, H, 3, CF], bf16)
        Sv = sb("Sv", [P, NJ, H, 2, CF], fp16)
        Rb = sb("Rb", [P, H + 1, CI])
        adj_rows = sb("adj_rows", [P, ROWS, N], bf16)
        WT = [sb("WT0", [P, KC, E0]), sb("WT1", [P, KC, E1])]
        a_cols = sb("a_cols", [P, KC, 2 + 2 * H])
        b_col = sb("b_col", [P, KC])
        bias = sb("bias", [P, E1])
        ident = sb("ident", [P, P])
        identb = sb("identb", [P, P], bf16)
        mean_h = [sb("mean_h0", [P, E0]), sb("mean_h1", [P, E1])]
        ysum = sb("ysum", [P, 2, KC, NC])
        ysums = sb("ysums", [P, KC])
        stats = sb("stats", [P, 2, CH, 6])
        mv = sb("mv", [P, 2, CH, 2])
        var_eps = sb("var_eps", [P, 2, CH])
        neg_mean = sb("neg_mean", [P, 2, CH])
        half = sb("half", [P, CH])
        minus_half = sb("minus_half", [P, CH])
        minus_one = sb("minus_one", [P, CH])
        alone_now = sb("alone_now", [P, CH])
        rstd = sb("rstd", [P, 2, CH])
        shift = sb("shift", [P, 2, CH])
        w_norm = sb("w_norm", [P, KC])
        b_abs = sb("b_abs", [P, KC])
        f_bound = sb("f_bound", [P, KC])
        scale = sb("scale", [P, H])
        scale_inv = sb("scale_inv", [P, H])
        d_part = [sb("d_part0", [P, 1]), sb("d_part1", [P, H])]
        d_max = [sb("d_max0", [P, 1]), sb("d_max1", [P, H])]
        dd = [sb("dd0", [P, NJ, 1]), sb("dd1", [P, NJ, H])]
        ss = [sb("ss0", [P, NJ, 1]), sb("ss1", [P, NJ, H])]
        w = [sb("w0", [P, NJ, 1]), sb("w1", [P, NJ, H])]
        v = [sb("v0", [P, NJ, 1]), sb("v1", [P, NJ, H])]
        wv = sb("wv", [P, NJ, H])
        R = sb("R", [P, NJ, H + 1])
        Rs = sb("Rs", [P, NJ, H])
        R_now = sb("R_now", [P, CH, H + 1])
        alone = sb("alone", [P, NC, CH])
        denA = sb("denA", [P, CH])
        denB = sb("denB", [P, CH])

        accA = pb("accA", [P, CH, 512])
        accB = pb("accB", [P, 3, 512])
        misc_ps = pb("misc_ps", [P, 512])
        turn_ps = misc_ps[:, :].bitcast(bf16).rearrange("p (j i) -> p j i", j=8)
        S_AT = ((0, 0), (0, NS), (1, 0), (2, 0))
        N_AT = ((1, NS), (1, NS + NN), (2, NS), (2, NS + NN))

        names = """w_loaded consts prep_t prep_e bound x_loaded0 x_loaded1 x_loaded2 x_loaded3 adj0 adj1
            stats_done mv_ready ve_ready rstd_ready norm_ready y_ready yt_turned yt_ready feat_done feat_moved
            chain exp_ready scaled hv_ready s_made s_chain n_chain sw_ready sv_ready misc_done misc_used
            tile_ready tile_free c_ready c0_ready n_ready bits_ready bits_free mask_turned mask_ready
            a_moved a_den a_quot a_mean x1_ready mean_made mean_added b_moved b_sum b_den x2_ready
            out_done r_now passed setup""".split()
        S = {n: sem(n) for n in names}
        x_loaded = [S[f"x_loaded{t}"] for t in range(NC)]
        adj_loaded = [S[f"adj{r}"] for r in range(ROWS)]

        def heads_view(L, col):
            if L == 0:
                return S0[:, :, F + col:F + col + 1]
            return S1.rearrange("p j (h e) -> p j h e", h=H)[:, :, :, C + col]

        def layer_index(ph, L):
            return 2 * ph if L == 0 else 2 * ph - 1

        def misc_before(kind, ph):
            first = 3 + NC
            each = 3 + (2 + H) + (H + 1) * NC
            return 0 if kind == "A" else each * ph + (first - each)

        def misc_before_layer(kind, ph, L):
            return misc_before(kind, ph) + (2 + H if L == 0 and kind != "A" else 0)

        def misc_before_step(kind, ph, c):
            if kind == "A":
                return 3 + c
            if kind == "B":
                return misc_before(kind, ph) + (2 + H) + H * c
            return misc_before(kind, ph) + (5 + H) + (H + 1) * c

        def turned_before(kind, ph):
            return 2 * CH * CHUNKS if kind == "B" else 2 * CH * NC * ph + 2 * CH

        def r_now_before(kind, ph):
            return 0 if kind == "A" else (NC + 2) * ph + (NC + 1 - (NC + 2))

        def rb_for(kind, ph, c, unit):
            if kind == "A":
                return 3 + c
            if kind == "B":
                return misc_before(kind, ph) + H * c + (3 + unit)
            return misc_before(kind, ph) + (H + 1) * c + (5 + unit)

        def wait(eng, s, value):
            if not isinstance(value, int) or value > 0:
                eng.wait_ge(s, value)

        def wait_alone(eng, s, value):
            wait(eng, s, value)
            eng.sem_inc(S["passed"], 1)

        def phases(eng, features, steps):
            features("A", 0)
            with eng.Fori(0, NC) as c:
                steps("A", STEP_A, 0, c)
            with eng.Fori(1, B - 1) as ph:
                features("AB", ph)
                with eng.Fori(0, NC) as c:
                    steps("AB", STEP_AB, ph, c)
            features("AB", B - 1)
            with eng.Fori(0, NC - 2) as c:
                steps("AB", STEP_AB, B - 1, c)
            steps("AB", STEP_AB_NEXT_LAST, B - 1, NC - 2)
            steps("AB", STEP_AB_LAST, B - 1, NC - 1)
            features("B", B)
            with eng.Fori(0, NC) as c:
                steps("B", STEP_B, B, c)

        block = ctx.enter_context(nc.Block())

        @block.sync
        def _(sp):
            def load_x(m, t):
                return sp.dma_start(xb[:, m % XSLOTS, :, :],
                                    x_rows[m, :, :, :]).then_inc(x_loaded[t], 16)

            x_rows = x_in.rearrange("b (c k p) f -> (b c) p k f", k=CH, p=P)
            out_rows = out.rearrange("b (c k p) f -> (b c) p k f", k=CH, p=P)
            for L, Wd in enumerate((W0, W1)):
                sp.dma_start(Wn[:, L, :, :], Wd.rearrange("(k p) f -> p k f", p=P)).then_inc(S["w_loaded"], 16)
            sp.wait_ge(S["consts"], 1)
            with nc.allow_non_contiguous_dma("small vectors, once"):
                for col, a in enumerate((a0_dst, a0_src)):
                    sp.dma_start(a_cols[:, :, col], a.rearrange("(k p) -> p k", p=P)).then_inc(S["w_loaded"], 16)
                sp.dma_start(b_col[:, :], b1.rearrange("(k p) -> p k", p=P)).then_inc(S["w_loaded"], 16)
                for h in range(H):
                    p0, k = h * C % P, h * C // P
                    for which in range(2):
                        sp.dma_start(a_cols[p0:p0 + C, k, 2 + 2 * h + which],
                                     a1[h, (1 - which) * C:(2 - which) * C]).then_inc(S["w_loaded"], 16)
            sp.dma_start(bias[:, :].rearrange("p (h e) -> p h e", h=H)[:, :, 0:C],
                         b1.rearrange("(h c) -> h c", h=H).partition_broadcast(P)).then_inc(S["w_loaded"], 16)
            for m in range(XSLOTS):
                if m >= NC:
                    sp.wait_ge(x_loaded[m - NC], 16)
                load_x(m, m % NC)

            def store(m):
                sp.wait_ge(S["x2_ready"], H * m + (H + 1))
                sp.dma_start(out_rows[m, :, :, :], xb[:, m % XSLOTS, :, :]).then_inc(S["out_done"], 16)
                wait_alone(sp, S["out_done"], 16 * m + 16)

            with sp.Fori(0, B - 2) as b:
                for t in range(NC):
                    store(NC * b + t)
                    load_x(NC * b + (t + XSLOTS), t)
            with sp.Fori(NC * (B - 2), CHUNKS) as m:
                store(m)

        @block.gpsimd
        def _(pool):
            adj_view = adj.rearrange("b (q r p) n -> (b q) r p n", r=CH, p=P)

            def load_adj(q, r):
                wait(pool, S["mask_turned"], 2 * CH * q + 2 * (r - ROWS + 1))
                pool.dma_start(adj_rows[:, r % ROWS, :], adj_view[q, r, :, :]).then_inc(adj_loaded[r % ROWS], 16)

            pool.sem_inc(S["x1_ready"], 1)
            pool.sem_inc(S["x2_ready"], 1)
            pool.memset(a_cols[:, :, :], 0.0).then_inc(S["consts"], 1)
            for r in range(ROWS):
                load_adj(0, r)
            pool.memset(half[:, :], 0.5)
            pool.memset(minus_half[:, :], -0.5)
            pool.memset(minus_one[:, :], -1.0)
            pool.memset(R[:, :, :], 0.0)
            for t in (ident, identb):
                last = pool.memset(t[:, :], 0.0)
            last.then_inc(S["consts"], 1)
            pool.wait_ge(S["consts"], 2)
            for t in (ident, identb):
                last = pool.affine_select(out=t[:, :], in_=t[:, :], compare_op=ALU.not_equal, fill=1.0, base=0,
                                          pattern=[[-1, P]], channel_multiplier=1)
            last.then_inc(S["consts"], 1)
            pool.wait_ge(S["bound"], 1)
            pool.tensor_tensor(w_norm[:, :], w_norm[:, :], half[:, 0:KC], ALU.pow).then_inc(S["bound"], 1)
            pool.wait_ge(S["bound"], 4)
            pool.tensor_tensor(scale[:, :], scale_inv[:, :], minus_one[:, 0:H], ALU.pow).then_inc(S["bound"], 1)
            for r in range(ROWS, CH):
                load_adj(0, r)
            for r in range(ROWS):
                load_adj(1, r)

            def features(kind, ph):
                for L in {"A": (0,), "AB": (1, 0), "B": (1,)}[kind]:
                    first = NC * layer_index(ph, L)
                    for t in range(NC):
                        f, s = first + t, t % 2
                        pool.wait_ge(S["mv_ready"], f + 1)
                        wait_alone(pool, S["y_ready"], CH * (f - 1))
                        pool.tensor_scalar(var_eps[:, s, :], mv[:, s, :, 1], EPS, None, ALU.add)
                        pool.tensor_scalar(neg_mean[:, s, :], mv[:, s, :, 0], -1.0, None, ALU.mult)\
                            .then_inc(S["ve_ready"], 1)
                        pool.wait_ge(S["ve_ready"], f + 1)
                        pool.tensor_tensor(rstd[:, s, :], var_eps[:, s, :], minus_half[:, :], ALU.pow)\
                            .then_inc(S["rstd_ready"], 1)
                        pool.wait_ge(S["rstd_ready"], f + 1)
                        pool.tensor_tensor(shift[:, s, :], rstd[:, s, :], neg_mean[:, s, :], ALU.mult)\
                            .then_inc(S["norm_ready"], 1)
                if kind == "A":
                    return
                wait_alone(pool, S["exp_ready"], 4 * ph)
                pool.tensor_tensor(v[1][:, :, :], v[1][:, :, :],
                                   scale[:, :].unsqueeze(1).to_broadcast([P, NJ, H]), ALU.mult)
                pool.tensor_tensor(Rs[:, :, :], R[:, :, 0:H],
                                   scale_inv[:, :].unsqueeze(1).to_broadcast([P, NJ, H]), ALU.mult)\
                    .then_inc(S["scaled"], 1)
                wait_alone(pool, S["scaled"], ph)
                for t in range(NC):
                    js = slice(CH * t, CH * t + CH)
                    i = NC * (ph - 1) + t
                    raw = S1[:, js, :].rearrange("p j (h e) -> p (j h) e", h=H)[:, :, 0:CF]
                    parts = Sv[:, js, :, :, :].rearrange("p j h a e -> p (j h) a e")
                    wait_alone(pool, S["s_made"], i + 1)
                    vs = v[1][:, js, :].rearrange("p j h -> p (j h)").unsqueeze(2)
                    pool.tensor_tensor(raw, raw, vs.to_broadcast([P, CH * H, CF]), ALU.mult)\
                        .then_inc(S["n_chain"], 1)
                    wait_alone(pool, S["n_chain"], 3 * i + 1)
                    pool.tensor_copy(parts[:, :, 0, :], raw).then_inc(S["n_chain"], 1)
                    wait_alone(pool, S["n_chain"], 3 * i + 2)
                    pool.tensor_tensor(raw, raw, parts[:, :, 0, :], ALU.subtract).then_inc(S["n_chain"], 1)
                    wait_alone(pool, S["n_chain"], 3 * i + 3)
                    pool.tensor_scalar(parts[:, :, 1, :], raw, LOW, None, ALU.mult).then_inc(S["sv_ready"], 1)

            def steps(kind, events, ph, c):
                n = ph * NC + c
                if kind != "A":
                    x1 = xb[:, (n + NC) % XSLOTS, :, :].rearrange("p k (h c) -> p k h c", h=H)
                    prod = numA[:, :, 0:F].rearrange("p k (h c) -> p k h c", h=H)
                    mean = mean_h[1][:, :].rearrange("p (h e) -> p h e", h=H)[:, :, 0:C]
                    wait_alone(pool, S["sw_ready"], NC * ph)
                    for k in range(CH):
                        last = pool.tensor_tensor(prod[:, k, :, :], mean,
                                                  alone[:, c, k:k + 1].unsqueeze(2).to_broadcast([P, H, C]), ALU.mult)
                    last.then_inc(S["mean_made"], 1)
                    wait_alone(pool, S["mean_made"], n - (NC - 1))
                    for k in range(CH):
                        last = pool.tensor_tensor(x1[:, k, :, :], x1[:, k, :, :], prod[:, k, :, :], ALU.add)
                    last.then_inc(S["mean_added"], 1)
                    wait_alone(pool, S["mean_added"], n - (NC - 1))
                for e in events:
                    if e[0] == "EA":
                        xs = xb[:, n % XSLOTS, :, :]
                        wait_alone(pool, S["a_moved"], n + 2)
                        pool.tensor_scalar(alone_now[:, :], numA[:, :, F], 0.0, None, ALU.is_equal)
                        pool.tensor_scalar(denA[:, :], numA[:, :, F], TINY, None, ALU.max).then_inc(S["a_den"], 1)
                        wait_alone(pool, S["a_den"], 2 * n + 1)
                        pool.tensor_copy(alone[:, c, :], alone_now[:, :])
                        pool.tensor_tensor(denA[:, :], denA[:, :], minus_one[:, :], ALU.pow)\
                            .then_inc(S["a_den"], 1)
                        pool.wait_ge(S["a_den"], 2 * n + 2)
                        pool.tensor_tensor(numA[:, :, 0:F], numA[:, :, 0:F],
                                           denA[:, :].unsqueeze(2).to_broadcast([P, CH, F]), ALU.mult)\
                            .then_inc(S["a_quot"], 1)
                        pool.wait_ge(S["a_quot"], n + 1)
                        pool.tensor_tensor(xs, xs, numA[:, :, 0:F], ALU.add).then_inc(S["a_mean"], 1)
                        wait_alone(pool, S["a_mean"], 2 * n + 1)
                        for k in range(CH):
                            last = pool.tensor_tensor(numA[:, k, 0:F], mean_h[0][:, 0:F],
                                                      alone_now[:, k:k + 1].to_broadcast([P, F]), ALU.mult)
                        last.then_inc(S["a_mean"], 1)
                        wait_alone(pool, S["a_mean"], 2 * n + 2)
                        pool.tensor_tensor(xs, xs, numA[:, :, 0:F], ALU.add).then_inc(S["x1_ready"], 1)
                    elif e[0] == "EB":
                        h = e[1]
                        g = H * (n - NC) + h
                        xs = xb[:, (n + NC) % XSLOTS, :, h * C:(h + 1) * C]
                        ns, nn = numS[:, :, 0:CF], numN[:, :, 0:CF]

                        def done(i):
                            wait_alone(pool, S["b_sum"], 6 * g + (i + 1))

                        wait_alone(pool, S["b_moved"], g + 2)
                        low = numN[:, :, CF:2 * CF]
                        pool.tensor_scalar(low, low, 1 / LOW, None, ALU.mult)
                        pool.tensor_tensor(ns, ns, numS[:, :, CF:2 * CF], ALU.add).then_inc(S["b_sum"], 1)
                        done(0)
                        pool.tensor_tensor(nn, nn, low, ALU.add)
                        pool.tensor_tensor(ns, ns, numS[:, :, 2 * CF:3 * CF], ALU.add).then_inc(S["b_sum"], 1)
                        done(1)
                        r_rows = Rs[:, :, :].rearrange("p (c k) h -> p c k h", k=CH)[:, c, :, h:h + 1]
                        pool.tensor_tensor(nn, nn, r_rows.to_broadcast([P, CH, CF]), ALU.mult)\
                            .then_inc(S["b_sum"], 1)
                        done(2)
                        pool.tensor_tensor(ns, ns, nn, ALU.add).then_inc(S["b_sum"], 1)
                        done(3)
                        pool.tensor_scalar(denB[:, :], ns[:, :, C], TINY, None, ALU.max).then_inc(S["b_sum"], 1)
                        done(4)
                        pool.tensor_tensor(denB[:, :], denB[:, :], minus_one[:, :], ALU.pow)\
                            .then_inc(S["b_sum"], 1)
                        done(5)
                        pool.tensor_tensor(ns[:, :, 0:C], ns[:, :, 0:C],
                                           denB[:, :].unsqueeze(2).to_broadcast([P, CH, C]), ALU.mult)\
                            .then_inc(S["b_den"], 1)
                        wait_alone(pool, S["b_den"], g + 1)
                        pool.tensor_tensor(xs, xs, ns[:, :, 0:C], ALU.add).then_inc(S["x2_ready"], 1)
                    elif e[0] == "L":
                        load_adj(n + e[1], e[2])

            phases(pool, features, steps)

        @block.scalar
        def _(act):
            act.sem_inc(S["a_moved"], 1)
            act.sem_inc(S["b_moved"], 1)
            for L in range(2):
                for k in range(KC):
                    i = 2 * (KC * L + k)
                    act.wait_ge(S["prep_t"], i + 1)
                    src = accA[:, 0, 0:F]
                    if L == 0:
                        nc.scalar.activation(WT[0][:, k, 0:F], src, ACT.Copy).then_inc(S["prep_e"], 1)
                    else:
                        nc.scalar.activation(WT[1][:, k, :].rearrange("p (h e) -> p h e", h=H)[:, :, 0:C],
                                             src.rearrange("p (h c) -> p h c", h=H), ACT.Copy)\
                            .then_inc(S["prep_e"], 1)
                    act.wait_ge(S["prep_t"], i + 2)
                    if L == 0:
                        nc.scalar.activation(WT[0][:, k, F:F + 2], accA[:, 1, 0:2], ACT.Copy)\
                            .then_inc(S["prep_e"], 1)
                    else:
                        nc.scalar.activation(WT[1][:, k, :].rearrange("p (h e) -> p h e", h=H)[:, :, C:C + 2],
                                             accA[:, 1, 0:2 * H].rearrange("p (h e) -> p h e", h=H), ACT.Copy)\
                            .then_inc(S["prep_e"], 1)
            act.wait_ge(S["prep_t"], 4 * KC + 1)
            nc.scalar.activation(bias[:, :].rearrange("p (h e) -> p h e", h=H)[:, :, C:C + 2],
                                 accA[:, 2, 0:2 * H].rearrange("p (h e) -> p h e", h=H), ACT.Copy)\
                .then_inc(S["prep_e"], 1)

            def move_mask(q, r, half_):
                act.wait_ge(S["mask_turned"], 2 * CH * q + (2 * r + half_ + 1))
                nc.scalar.activation(mask[:, q % MSLOTS, 8 * half_:8 * half_ + 8, r * P:(r + 1) * P],
                                     turn_ps[:, :, :], ACT.Copy, scale=MARK).then_inc(S["mask_ready"], 1)

            def move_rb(misc, unit):
                act.wait_ge(S["misc_done"], misc + 1)
                nc.scalar.activation(Rb[:, unit, :], misc_ps[:, :], ACT.Copy).then_inc(S["misc_used"], 1)

            for r in range(CH):
                for half_ in range(2):
                    move_mask(0, r, half_)

            def features(kind, ph):
                def norm(L, t):
                    f, s = NC * layer_index(ph, L) + t, t % 2
                    act.wait_ge(S["norm_ready"], f + 1)
                    wait(act, S["yt_turned"], f - 1)
                    for k in range(CH):
                        nc.scalar.activation(y[:, s, k, :], xb[:, (NC * (ph - L) + t) % XSLOTS, k, :], ACT.Relu,
                                             bias=shift[:, s, k:k + 1], scale=rstd[:, s, k:k + 1])\
                            .then_inc(S["y_ready"], 1)

                def move_yt(L, t):
                    f, s = NC * layer_index(ph, L) + t, t % 2
                    act.wait_ge(S["yt_turned"], f + 1)
                    wait(act, S["feat_done"], CH * (f - 1))
                    for k in range(KC):
                        nc.scalar.activation(yT[:, s, k, :], accA[:, k, :], ACT.Copy,
                                             accum_out=ysum[:, L, k, t:t + 1]).then_inc(S["yt_ready"], 1)

                def move_features(t):
                    for k in range(CH):
                        g = CH * (NC * layer_index(ph, 0) + t) + k
                        act.wait_ge(S["feat_done"], g + 1)
                        nc.scalar.activation(S0[:, CH * t + k, :], accA[:, 2 + k % 2, 0:E0], ACT.Copy)\
                            .then_inc(S["feat_moved"], 1)

                def exps(L):
                    i = layer_index(ph, L)
                    act.wait_ge(S["chain"], 4 * i + 4)
                    nc.scalar.activation(v[L][:, :, :], dd[L][:, :, :], ACT.Exp, scale=LEAKY)\
                        .then_inc(S["exp_ready"], 1)
                    if L == 1:
                        nc.scalar.activation(wv[:, :, :], dd[1][:, :, :], ACT.Exp)
                    nc.scalar.activation(w[L][:, :, :], dd[L][:, :, :], ACT.Exp, scale=1 - LEAKY)
                    col = slice(H, H + 1) if L == 0 else slice(0, H)
                    nc.scalar.activation(R[:, :, col], ss[L][:, :, :], ACT.Exp, scale=-(1 - LEAKY))\
                        .then_inc(S["exp_ready"], 1)
                    act.wait_ge(S["exp_ready"], 2 * i + 2)
                    nc.scalar.activation(R_now[:, :, col], R[:, 0:CH, col], ACT.Copy).then_inc(S["r_now"], 1)

                m1, m0 = misc_before_layer(kind, ph, 1) + 2, misc_before_layer(kind, ph, 0) + 2
                if kind != "A":
                    wait(act, S["n_ready"], NR + HG * (NC * ph - NC))
                    norm(1, 0)
                    move_yt(1, 0)
                    wait(act, S["x1_ready"], NC * ph + 1)
                    norm(1, 1)
                    for t in range(1, NC):
                        move_yt(1, t)
                        if t + 1 < NC:
                            norm(1, t + 1)
                        elif kind == "AB":
                            norm(0, 0)
                if kind == "A":
                    norm(0, 0)
                if kind == "B":
                    exps(1)
                    for unit in range(H):
                        move_rb(m1 + unit, unit)
                    return
                move_yt(0, 0)
                norm(0, 1)
                move_yt(0, 1)
                norm(0, 2)
                move_features(0)
                if kind == "AB":
                    exps(1)
                move_yt(0, 2)
                norm(0, 3)
                move_features(1)
                if kind == "AB":
                    move_rb(m1, 0)
                    move_rb(m1 + 1, 1)
                move_yt(0, 3)
                move_features(2)
                if kind == "AB":
                    move_rb(m1 + 2, 2)
                    move_rb(m1 + 3, 3)
                move_features(3)
                exps(0)
                move_rb(m0, H)

            def steps(kind, events, ph, c):
                n = ph * NC + c
                misc = misc_before_step(kind, ph, c)
                first_r = True

                def compare(i):
                    h, g, slot = i // G, i % G, i % CRING
                    if g == 0:
                        act.wait_ge(S["misc_used"], rb_for(kind, ph, c, h))
                    skipped = 0 if i - CRING >= G else G
                    act.wait_ge(S["n_ready"], HG * (n - NC) + (NR + i - CRING + 1 - skipped))
                    for jj in range(JG):
                        last = nc.scalar.activation(cmp[:, slot, jj, :], Rb[:, h, :], ACT.Sign,
                                                    bias=w[1][:, JG * g + jj, h:h + 1], scale=-1.0)
                    last.then_inc(S["c_ready"], 1)

                for e in events:
                    if e[0] == "M":
                        move_mask(n + 1, e[1], e[2])
                    elif e[0] == "R":
                        if first_r:
                            nc.scalar.activation(R_now[:, :, :],
                                                 R[:, :, :].rearrange("p (c k) u -> p c k u", k=CH)[:, (c + 1) % NC, :, :],
                                                 ACT.Copy).then_inc(S["r_now"], 1)
                            first_r = False
                        if e[1] == H:
                            act.wait_ge(S["tile_ready"], NJ * n + NJ)
                        elif e[1] == 0:
                            act.wait_ge(S["c0_ready"], G * (n - NC) + G)
                        else:
                            act.wait_ge(S["c_ready"], CG * (n - NC) + G * e[1])
                        move_rb(misc, e[1])
                        misc = misc + 1
                    elif e[0] == "G":
                        i = G * e[1] + e[2] + LEAD
                        if G <= i < HG:
                            compare(i)
                    elif e[0] == "EA":
                        act.wait_ge(S["tile_free"], NJ * n + (RING + NJ))
                        act.wait_ge(S["x1_ready"], n + 1)
                        if kind != "A":
                            act.wait_ge(S["mean_added"], n - (NC - 1))
                        nc.scalar.activation(numA[:, :, :], accA[:, :, 0:F + 1], ACT.Copy)\
                            .then_inc(S["a_moved"], 1)
                    elif e[0] == "EB":
                        h = e[1]
                        act.wait_ge(S["bits_free"], HG * (n - NC) + (BRING + G * h + G))
                        act.wait_ge(S["x2_ready"], H * (n - NC) + (h + 1))
                        nc.scalar.activation(numS[:, 0:2, :].rearrange("p k e -> p (k e)"), accB[:, 0, 0:2 * NS],
                                             ACT.Copy)
                        nc.scalar.activation(numS[:, 2:4, :], accB[:, 1:3, 0:NS], ACT.Copy)
                        nc.scalar.activation(numN.rearrange("p (b k) e -> p b (k e)", b=2),
                                             accB[:, 1:3, NS:NS + 2 * NN], ACT.Copy).then_inc(S["b_moved"], 1)

            phases(act, features, steps)

        @block.tensor
        def _(pe):
            pe.wait_ge(S["consts"], 3)
            pe.wait_ge(S["w_loaded"], 16 * (6 + 2 * H))
            for L in range(2):
                acols = a_cols[:, :, 0:2] if L == 0 else a_cols[:, :, 2:2 + 2 * H]
                na = 2 * HEADS[L]
                for k in range(KC):
                    i = 2 * (KC * L + k)
                    wait(pe, S["prep_e"], i)
                    for o in range(KC):
                        last = nc.tensor.transpose(accA[:, 0, o * P:(o + 1) * P],
                                                   Wn[:, L, o, k * P:(k + 1) * P], ident[:, :])
                    last.then_inc(S["prep_t"], 1)
                    for o in range(KC):
                        last = nc.tensor.matmul(accA[:, 1, 0:na], Wn[:, L, o, k * P:(k + 1) * P],
                                                acols[:, o, :], start=o == 0, stop=o == KC - 1)
                    last.then_inc(S["prep_t"], 1)
            for o in range(KC):
                last = nc.tensor.matmul(accA[:, 2, 0:2 * H], b_col[:, o:o + 1].to_broadcast([P, P]),
                                        a_cols[:, o, 2:2 + 2 * H], start=o == 0, stop=o == KC - 1)
            last.then_inc(S["prep_t"], 1)
            pe.wait_ge(S["bound"], 3)
            for o in range(KC):
                last = nc.tensor.transpose(accA[:, 3, o * P:(o + 1) * P],
                                           f_bound[:, o:o + 1].to_broadcast([P, P]), ident[:, :])
            last.then_inc(S["prep_t"], 1)
            pe.wait_ge(S["prep_e"], 4 * KC + 1)

            def turn_mask(q, r, half_, misc):
                if half_ == 0:
                    pe.wait_ge(adj_loaded[r % ROWS], 16 * (CH // ROWS) * q + 16 * (r // ROWS + 1))
                wait(pe, S["mask_ready"], 2 * CH * q + (2 * r + half_))
                wait(pe, S["misc_used"], misc)
                for j in range(8):
                    col = (8 * half_ + j) * P
                    last = nc.tensor.transpose(turn_ps[:, j, :], adj_rows[:, r % ROWS, col:col + P], identb[:, :])
                last.then_inc(S["mask_turned"], 1)

            def turn_r(misc, unit, turned):
                wait(pe, S["misc_used"], misc)
                wait(pe, S["mask_ready"], turned)
                for k in range(CH):
                    last = nc.tensor.transpose(misc_ps[:, k * P:(k + 1) * P],
                                               R_now[:, k, unit:unit + 1].to_broadcast([P, P]), ident[:, :])
                last.then_inc(S["misc_done"], 1)

            for r in range(CH):
                for half_ in range(2):
                    turn_mask(0, r, half_, 0)

            def features(kind, ph):
                def turn_y(L, t):
                    f, s = NC * layer_index(ph, L) + t, t % 2
                    wait(pe, S["yt_ready"], 2 * f)
                    for k in range(CH):
                        pe.wait_ge(S["y_ready"], CH * f + (k + 1))
                        for kc in range(KC):
                            last = nc.tensor.transpose(accA[:, kc, k * P:(k + 1) * P],
                                                       y[:, s, k, kc * P:(kc + 1) * P], ident[:, :])
                    last.then_inc(S["yt_turned"], 1)

                def feats(L, t):
                    f, s = NC * layer_index(ph, L) + t, t % 2
                    pe.wait_ge(S["yt_ready"], 2 * f + 2)
                    for k in range(CH):
                        g = CH * f + k
                        wait(pe, S["feat_moved"], g - 1)
                        for kc in range(KC):
                            last = nc.tensor.matmul(accA[:, 2 + k % 2, 0:COLS[L]], yT[:, s, kc, k * P:(k + 1) * P],
                                                    WT[L][:, kc, :], start=kc == 0, stop=kc == KC - 1)
                        last.then_inc(S["feat_done"], 1)

                def turn_max(L):
                    i, m = layer_index(ph, L), misc_before_layer(kind, ph, L)
                    pe.wait_ge(S["chain"], 4 * i + 1)
                    wait(pe, S["misc_used"], m)
                    wait(pe, S["mask_ready"], turned_before(kind, ph))
                    for h in range(HEADS[L]):
                        last = nc.tensor.transpose(misc_ps[:, h * P:(h + 1) * P],
                                                   d_part[L][:, h:h + 1].to_broadcast([P, P]), ident[:, :])
                    last.then_inc(S["misc_done"], 1)

                def mean(L):
                    i, m = layer_index(ph, L), misc_before_layer(kind, ph, L)
                    pe.wait_ge(S["chain"], 4 * i + 2)
                    pe.wait_ge(S["misc_used"], m + 1)
                    for kc in range(KC):
                        last = nc.tensor.matmul(misc_ps[:, 0:COLS[L]], ysums[:, kc:kc + 1].to_broadcast([P, P]),
                                                WT[L][:, kc, :], start=kc == 0, stop=kc == KC - 1)
                    last.then_inc(S["misc_done"], 1)

                def first_r(L, units):
                    pe.wait_ge(S["r_now"], r_now_before(kind, ph) + (1 if L == 1 or kind == "A" else 2))
                    for unit in units:
                        turn_r(misc_before_layer(kind, ph, L) + (2 + (unit if L == 1 else 0)), unit, 0)

                if kind != "A":
                    pe.wait_ge(S["a_moved"], ph * NC + 1)
                    turn_y(1, 0)
                    for t in range(NC):
                        if t + 1 < NC:
                            turn_y(1, t + 1)
                        feats(1, t)
                if kind == "B":
                    turn_max(1)
                    mean(1)
                    first_r(1, range(H))
                    return
                turn_y(0, 0)
                turn_y(0, 1)
                feats(0, 0)
                if kind == "AB":
                    turn_max(1)
                    mean(1)
                turn_y(0, 2)
                feats(0, 1)
                if kind == "AB":
                    first_r(1, (0, 1))
                turn_y(0, 3)
                feats(0, 2)
                if kind == "AB":
                    first_r(1, (2, 3))
                feats(0, 3)
                turn_max(0)
                mean(0)
                first_r(0, (H,))
                wait_alone(pe, S["hv_ready"], NC * ph + NC)

            def steps(kind, events, ph, c):
                n = ph * NC + c
                misc = misc_before_step(kind, ph, c)
                turned = 2 * CH * CHUNKS if kind == "B" else 2 * CH * n + 2 * CH
                first_r = True
                for e in events:
                    if e[0] == "A":
                        j = e[1]
                        if j == 0:
                            pe.wait_ge(S["a_moved"], n + 1)
                        pe.wait_ge(S["tile_ready"], NJ * n + (j + 1))
                        for k in range(CH):
                            last = nc.tensor.matmul(accA[:, k, 0:F + 1], tiles[:, j % RING, k * P:(k + 1) * P],
                                                    S0[:, j, 0:F + 1], start=j == 0, stop=j == NJ - 1)
                        last.then_inc(S["tile_free"], 1)
                    elif e[0] == "G":
                        h, g = e[1:]
                        if g == 0:
                            if h == 0:
                                pe.wait_ge(S["sw_ready"], NC * ph)
                                pe.wait_ge(S["sv_ready"], NC * ph)
                            pe.wait_ge(S["b_moved"], H * (n - NC) + (h + 1))
                        wait_alone(pe, S["bits_ready"], HG * (n - NC) + (G * h + g + 1))
                        for jj in range(JG):
                            j = JG * g + jj
                            for k in range(CH):
                                bank, col = S_AT[k]
                                nc.tensor.matmul(accB[:, bank, col:col + NS],
                                                 bits[:, g % BRING, 1, jj, k * P:(k + 1) * P],
                                                 Sw[:, j, h, :, :].rearrange("p a e -> p (a e)"),
                                                 start=j == 0 and col == 0, stop=j == NJ - 1, skip_group_check=True)
                            for k in range(CH):
                                bank, col = N_AT[k]
                                last = nc.tensor.matmul(accB[:, bank, col:col + NN],
                                                        bits[:, g % BRING, 0, jj, k * P:(k + 1) * P],
                                                        Sv[:, j, h, :, :].rearrange("p a e -> p (a e)"),
                                                        start=False, stop=j == NJ - 1, skip_group_check=True)
                        last.then_inc(S["bits_free"], 1)
                    elif e[0] == "M":
                        turn_mask(n + 1, e[1], e[2], misc)
                        turned = turned + 1
                    elif e[0] == "R":
                        if first_r:
                            pe.wait_ge(S["r_now"], r_now_before(kind, ph) + c + (3 if kind == "AB" else 2))
                            first_r = False
                        turn_r(misc, e[1], turned)
                        misc = misc + 1

            phases(pe, features, steps)

        @block.vector
        def _(dve):
            dve.sem_inc(S["tile_free"], RING)
            dve.sem_inc(S["bits_free"], BRING)
            dve.sem_inc(S["n_ready"], NR)
            dve.wait_ge(S["w_loaded"], 16 * (6 + 2 * H))
            nc.vector.tensor_tensor(squares, Wn[:, 1, :, :], Wn[:, 1, :, :], ALU.mult).then_inc(S["setup"], 1)
            nc.vector.scalar_tensor_tensor(out=b_abs[:, :], in0=b_col[:, :], scalar=-1.0, in1=b_col[:, :],
                                           op0=ALU.mult, op1=ALU.max).then_inc(S["setup"], 1)
            dve.wait_ge(S["setup"], 2)
            nc.vector.tensor_reduce(w_norm[:, :], squares, AX.X, ALU.add).then_inc(S["bound"], 1)
            dve.wait_ge(S["bound"], 2)
            nc.vector.scalar_tensor_tensor(out=f_bound[:, :], in0=w_norm[:, :], scalar=float(F) ** 0.5,
                                           in1=b_abs[:, :], op0=ALU.mult, op1=ALU.add).then_inc(S["bound"], 1)
            dve.wait_ge(S["prep_t"], 4 * KC + 2)
            nc.vector.tensor_reduce(scale_inv[:, :], accA[:, 3, 0:F].rearrange("p (h c) -> p h c", h=H),
                                    AX.X, ALU.max).then_inc(S["setup"], 1)
            dve.wait_ge(S["setup"], 3)
            nc.vector.tensor_scalar(scale_inv[:, :], scale_inv[:, :], 1.0, 2.0 ** -14, ALU.max, ALU.mult)\
                .then_inc(S["bound"], 1)

            def features(kind, ph):
                def statistics(L, t):
                    f, s = NC * layer_index(ph, L) + t, t % 2
                    b = ph - L
                    xs = xb[:, (NC * b + t) % XSLOTS, :, :]
                    if L == 0:
                        dve.wait_ge(x_loaded[t], 16 * b + 16)
                    else:
                        dve.wait_ge(S["x1_ready"], NC * b + (t + 2))
                    wait_alone(dve, S["norm_ready"], f - 1)
                    for k in range(CH):
                        last = nc.vector.bn_stats(stats[:, s, k, :], xs[:, k, :])
                    last.then_inc(S["stats_done"], 1)
                    wait_alone(dve, S["stats_done"], f + 1)
                    for k in range(CH):
                        last = nc.vector.bn_aggr(mv[:, s, k, :], stats[:, s, k, :])
                    last.then_inc(S["mv_ready"], 1)

                def move_features(t):
                    for k in range(CH):
                        g = CH * (NC * layer_index(ph, 1) + t) + k
                        dve.wait_ge(S["feat_done"], g + 1)
                        nc.vector.tensor_tensor(S1[:, CH * t + k, :], accA[:, 2 + k % 2, 0:E1], bias[:, :], ALU.add)\
                            .then_inc(S["feat_moved"], 1)

                def maxima(L):
                    first = NC * layer_index(ph, L)
                    dve.wait_ge(S["feat_moved"], CH * (first + NC))
                    nc.vector.tensor_reduce(d_part[L][:, :], heads_view(L, 0).rearrange("p j h -> p h j"),
                                            AX.X, ALU.max).then_inc(S["chain"], 1)
                    dve.wait_ge(S["yt_ready"], 2 * (first + NC))
                    if L == 0 and kind == "AB":
                        dve.wait_ge(S["misc_done"], misc_before_layer(kind, ph, 1) + 2)
                    nc.vector.tensor_reduce(ysums[:, :], ysum[:, L, :, :], AX.X, ALU.add).then_inc(S["chain"], 1)

                def shifted(L):
                    i, m, nh = layer_index(ph, L), misc_before_layer(kind, ph, L), HEADS[L]
                    dve.wait_ge(S["misc_done"], m + 1)
                    nc.vector.tensor_reduce(d_max[L][:, :], misc_ps[:, 0:nh * P].rearrange("p (h n) -> p h n", h=nh),
                                            AX.X, ALU.max).then_inc(S["misc_used"], 1)
                    dve.wait_ge(S["misc_used"], m + 1)
                    dmax_b = d_max[L][:, :].unsqueeze(1).to_broadcast([P, NJ, nh])
                    nc.vector.tensor_tensor(dd[L][:, :, :], heads_view(L, 0), dmax_b, ALU.subtract)
                    nc.vector.tensor_tensor(ss[L][:, :, :], heads_view(L, 1), dmax_b, ALU.add).then_inc(S["chain"], 1)
                    dve.wait_ge(S["chain"], 4 * i + 3)
                    nc.vector.tensor_scalar(ss[L][:, :, :], ss[L][:, :, :], 0.0, None, ALU.max)\
                        .then_inc(S["chain"], 1)
                    dve.wait_ge(S["misc_done"], m + 2)
                    if L == 0:
                        nc.vector.tensor_scalar(mean_h[0][:, :], misc_ps[:, 0:E0], 1.0 / N, None, ALU.mult)\
                            .then_inc(S["misc_used"], 1)
                    else:
                        nc.vector.memset(heads_view(1, 0), 1.0)
                        nc.vector.scalar_tensor_tensor(out=mean_h[1][:, :], in0=misc_ps[:, 0:E1], scalar=1.0 / N,
                                                       in1=bias[:, :], op0=ALU.mult, op1=ALU.add)\
                            .then_inc(S["misc_used"], 1)

                def scale_features():
                    dve.wait_ge(S["exp_ready"], 4 * ph + 1)
                    for t in range(NC):
                        for j in range(CH * t, CH * t + CH):
                            nc.vector.tensor_scalar(S0[:, j, 0:F], S0[:, j, 0:F], v[0][:, j, :], None, ALU.mult)
                        js = slice(CH * t, CH * t + CH)
                        nc.vector.tensor_copy(S0[:, js, F:F + 1], v[0][:, js, :]).then_inc(S["hv_ready"], 1)

                def split_features(t):
                    js = slice(CH * t, CH * t + CH)
                    i = NC * (ph - 1) + t
                    raw = S1[:, js, :].rearrange("p j (h e) -> p (j h) e", h=H)[:, :, 0:CF]
                    parts = Sw[:, js, :, :, :].rearrange("p j h a e -> p (j h) a e")
                    if t == 0:
                        dve.wait_ge(S["misc_used"], misc_before_layer(kind, ph, 1) + 2)
                        dve.wait_ge(S["exp_ready"], 4 * ph)
                        dve.wait_ge(S["x2_ready"], H * NC * (ph - 1) + 1)
                    else:
                        dve.wait_ge(S["sw_ready"], i)
                    ws = wv[:, js, :].rearrange("p j h -> p (j h)").unsqueeze(2)
                    nc.vector.tensor_tensor(split, raw, ws.to_broadcast([P, CH * H, CF]), ALU.mult)\
                        .then_inc(S["s_made"], 1)
                    dve.wait_ge(S["s_made"], i + 1)
                    nc.vector.tensor_copy(parts[:, :, 0, :], split).then_inc(S["s_chain"], 1)
                    dve.wait_ge(S["s_chain"], 3 * i + 1)
                    nc.vector.tensor_tensor(split, split, parts[:, :, 0, :], ALU.subtract).then_inc(S["s_chain"], 1)
                    dve.wait_ge(S["s_chain"], 3 * i + 2)
                    nc.vector.tensor_copy(parts[:, :, 1, :], split).then_inc(S["s_chain"], 1)
                    dve.wait_ge(S["s_chain"], 3 * i + 3)
                    nc.vector.tensor_tensor(parts[:, :, 2, :], split, parts[:, :, 1, :], ALU.subtract)\
                        .then_inc(S["sw_ready"], 1)

                if kind != "A":
                    for t in range(NC):
                        statistics(1, t)
                    move_features(0)
                    if kind == "AB":
                        statistics(0, 0)
                    move_features(1)
                    if kind == "AB":
                        statistics(0, 1)
                    move_features(2)
                    move_features(3)
                    maxima(1)
                    if kind == "AB":
                        statistics(0, 2)
                    shifted(1)
                    if kind == "AB":
                        statistics(0, 3)
                    for t in range(NC if kind == "B" else 2):
                        split_features(t)
                else:
                    for t in range(NC):
                        statistics(0, t)
                if kind != "B":
                    maxima(0)
                    shifted(0)
                    scale_features()
                if kind == "AB":
                    for t in range(2, NC):
                        split_features(t)

            def steps(kind, events, ph, c):
                n = ph * NC + c
                first_compare = True
                for e in vector_order(events):
                    if e[0] == "A":
                        j = e[1]
                        if j == 0:
                            dve.wait_ge(S["misc_used"], rb_for(kind, ph, c, H if kind != "A" else 0))
                            dve.wait_ge(S["mask_ready"], 2 * CH * n + 2 * CH)
                        if j % 2 == 0:
                            dve.wait_ge(S["tile_free"], NJ * n + (j + 2))
                        nc.vector.scalar_tensor_tensor(out=tiles[:, j % RING, :], in0=Rb[:, H, :],
                                                       scalar=w[0][:, j, :], in1=mask[:, n % MSLOTS, j, :],
                                                       op0=ALU.max, op1=ALU.mult).then_inc(S["tile_ready"], 1)
                        continue
                    if e[0] == "C0":
                        if first_compare:
                            first_compare = False
                            dve.wait_ge(S["misc_used"], rb_for(kind, ph, c, 0))
                            dve.wait_ge(S["sv_ready"], NC * ph)
                        for jj in range(JG):
                            last = nc.vector.tensor_scalar(c0[:, jj, :], Rb[:, 0, :],
                                                           w[1][:, JG * e[1] + jj, 0:1], 255.0, ALU.is_gt, ALU.mult)
                        last.then_inc(S["c0_ready"], 1)
                        continue
                    h, g = e[1:]
                    slot = g % BRING
                    chunk_mask = mask[:, (n - NC) % MSLOTS, JG * g:JG * g + JG, :].bitcast(u32)
                    n_bits, s_bits = bits[:, slot, 0, :, :].bitcast(u32), bits[:, slot, 1, :, :].bitcast(u32)
                    i = G * h + g
                    if e[0] == "N":
                        if h == 0:
                            dve.wait_ge(S["c0_ready"], G * (n - NC) + (g + 1))
                            src = c0
                        else:
                            dve.wait_ge(S["c_ready"], CG * (n - NC) + (i - G + 1))
                            src = cmp[:, i % CRING, :, :]
                        dve.wait_ge(S["bits_free"], HG * (n - NC) + (i + 1))
                        nc.vector.tensor_tensor(n_bits, src.bitcast(u32), chunk_mask, ALU.bitwise_and)\
                            .then_inc(S["n_ready"], 1)
                    else:
                        dve.wait_ge(S["n_ready"], HG * (n - NC) + (NR + i + 1))
                        nc.vector.tensor_tensor(s_bits, n_bits, chunk_mask, ALU.bitwise_xor)\
                            .then_inc(S["bits_ready"], 1)

            phases(dve, features, steps)


def kernel(x, adj, L0_gnn_W, L0_gnn_a_src, L0_gnn_a_dst, L1_gnn_W, L1_gnn_b, L1_gnn_a):
    import numpy as np
    import concourse.bacc as bacc
    from concourse.bass_utils import run_bass_kernel_spmd

    nc = bacc.Bacc("TRN2", target_bir_lowering=False, num_devices=1)
    given = dict(x=x, adj=adj, W0=L0_gnn_W, a0_src=L0_gnn_a_src, a0_dst=L0_gnn_a_dst,
                 W1=L1_gnn_W, b1=L1_gnn_b, a1=L1_gnn_a)
    arrays = {f"in_{name}": np.ascontiguousarray(a) for name, a in given.items()}
    args = [nc.dram_tensor(name, a.shape, mybir.dt.from_np(a.dtype), kind="ExternalInput").ap()
            for name, a in arrays.items()]
    out = nc.dram_tensor("out", arrays["in_x"].shape, mybir.dt.float32, kind="ExternalOutput").ap()
    gat_two_layers(nc, *args, out)
    return run_bass_kernel_spmd(nc, [arrays], core_ids=[0]).results[0]["out"]
```

```python
import concourse.bass as bass
from concourse import mybir
from contextlib import ExitStack


def gat_two_layers(nc: bass.Bass, x_in: bass.AP, adj: bass.AP, W0: bass.AP, a0_src: bass.AP, a0_dst: bass.AP,
                   W1: bass.AP, b1: bass.AP, a1: bass.AP, out: bass.AP):
    fp32, bf16, fp16 = mybir.dt.float32, mybir.dt.bfloat16, mybir.dt.float16
    u8, i8, u32, fp8 = mybir.dt.uint8, mybir.dt.int8, mybir.dt.uint32, mybir.dt.float8e4
    ALU, ACT, AX = mybir.AluOpType, mybir.ActivationFunctionType, mybir.AxisListType

    B, N, F = x_in.shape
    P = 128
    KC = F // P
    NJ = N // P
    CH = 4
    NC = NJ // CH
    CI = CH * P
    H = a1.shape[0]
    C = F // H
    E0 = F + 2
    EH = C + 2
    E1 = H * EH
    HEADS = (1, H)
    COLS = (E0, E1)
    RING = 4
    JG = 4
    G = NJ // JG
    HG = H * G
    BRING = 4
    CRING = 2
    AB_GROUPS = [0, 1]
    B_GROUPS = [0, 1, 4, 7, 10, 13]
    LEAD = 4
    CF = C + 1
    NS, NN = 3 * CF, 2 * CF
    ROWS = 2
    MARK = 64.0
    LOW = 2.0 ** 11
    LEAKY = 0.2
    EPS = 1e-5
    TINY = 1.2e-38
    CHUNKS = B * NC
    XSLOTS = 2 * NC
    MSLOTS = NC + 2

    def order(do_a, do_b, do_m, do_l):
        events = []
        for h in range(H):
            last = h == H - 1
            a = [("A", G * h + i) for i in range(G)] if do_a else [None] * G
            g = [("G", h, i) for i in range(G)] if do_b else [None] * G
            m = [("M", h, i) for i in range(2)] if do_m else [None] * 2
            load = [("L", 1 + (h + ROWS) // CH, (h + ROWS) % CH)] if (do_m if h + ROWS < CH else do_l) else []
            r = [("R", h)] if do_b else []
            ra = [("R", H)] if do_a and last else []
            ea = [("EA",)] if do_a and last else []
            x1 = [("X1", 0)] if do_a and do_b and last else []
            eb = [("EB", h)] if do_b else []
            if not last:
                events += [a[0], a[1], g[0], m[0], g[1], a[2], m[1]] + load + [g[2], a[3]] + r + [g[3]] + eb
            else:
                events += [a[0], a[1], m[0], a[2], a[3]] + ea + [g[0]] + ra + [g[1], m[1]] + load
                events += [g[2]] + r + [g[3]] + x1 + eb
        return [e for e in events if e]

    def compared(kind):
        vec = {"A": [], "AB": AB_GROUPS, "B": B_GROUPS}[kind]
        return vec, [i for i in range(HG) if i not in vec]

    def vector_order(kind, events):
        work = [e for e in events if e[0] in ("A", "G", "X1")]
        own = compared(kind)[0]
        out_order = []
        for i, e in enumerate(work):
            nxt = work[i + 1] if i + 1 < len(work) else None
            if e[0] == "A":
                if nxt and nxt[0] == "G" and G * nxt[1] + nxt[2] not in own:
                    out_order += [("N", nxt[1], nxt[2]), e, ("S", nxt[1], nxt[2])]
                else:
                    out_order += [e]
            elif e[0] == "X1":
                out_order += [e]
            elif ("N", e[1], e[2]) not in out_order:
                out_order += [("C0", e[1], e[2])] if G * e[1] + e[2] in own else []
                out_order += [("N", e[1], e[2]), ("S", e[1], e[2])]
            if e[0] == "G" and e[1:] == (1, 0):
                out_order += [("MEAN",)]
        return out_order

    step_a = order(1, 0, 1, 1)
    STEP_A_FIRST, STEP_A, STEP_A_END = step_a, step_a[:4] + [("X1", 1)] + step_a[4:], [("X1", 0)]
    STEP_AB, STEP_B = order(1, 1, 1, 1), order(0, 1, 0, 0)
    STEP_AB_NEXT_LAST, STEP_AB_LAST = order(1, 1, 1, 0), order(1, 1, 0, 0)
    NR = CRING

    ctx = ExitStack()
    with ctx:
        def sb(name, shape, dt=fp32):
            return ctx.enter_context(nc.sbuf_tensor(name, shape, dt))

        def pb(name, shape, dt=fp32):
            return ctx.enter_context(nc.psum_tensor(name, shape, dt))

        def sem(name):
            return ctx.enter_context(nc.semaphore(name))

        AT_TILES = max(BRING * 2 * JG * CI, NJ * E1 * 4)
        AT_C = AT_TILES + RING * CI * 4
        AT_NUMA = AT_C + CRING * JG * CI
        AT_NUMS = AT_NUMA + CH * (F + 1) * 4
        AT_NUMN = AT_NUMS + CH * NS * 4
        shared = sb("shared", [P, AT_NUMN + CH * NN * 4], u8)

        def part(at, size, dt):
            return shared[:, at:at + size].bitcast(dt)

        bits = part(0, BRING * 2 * JG * CI, fp8).rearrange("p (r t j i) -> p r t j i", r=BRING, t=2, j=JG)
        tiles = part(AT_TILES, RING * CI * 4, fp32).rearrange("p (r i) -> p r i", r=RING)
        cmp = part(AT_C, CRING * JG * CI, i8).rearrange("p (r j i) -> p r j i", r=CRING, j=JG)
        numA = part(AT_NUMA, CH * (F + 1) * 4, fp32).rearrange("p (k e) -> p k e", k=CH)
        numS = part(AT_NUMS, CH * NS * 4, fp32).rearrange("p (k e) -> p k e", k=CH)
        numN = part(AT_NUMN, CH * NN * 4, fp32).rearrange("p (k e) -> p k e", k=CH)
        S1 = part(0, NJ * E1 * 4, fp32).rearrange("p (j e) -> p j e", j=NJ)
        yT = part(AT_TILES, 2 * KC * CI * 4, fp32).rearrange("p (s k i) -> p s k i", s=2, k=KC)
        y = part(AT_C, 2 * CH * F * 4, fp32).rearrange("p (s k f) -> p s k f", s=2, k=CH)
        Wn = part(AT_TILES, 2 * KC * F * 4, fp32).rearrange("p (l k f) -> p l k f", l=2, k=KC)
        split = part(AT_NUMS, CH * H * CF * 4, fp32).rearrange("p (j e) -> p j e", e=CF)
        squares = part(AT_NUMS, KC * F * 4, fp32).rearrange("p (k f) -> p k f", k=KC)
        assert AT_C + 2 * CH * F * 4 <= AT_NUMS
        assert 2 * CI <= E1 * 4

        c0 = sb("c0", [P, JG, CI], u8)
        mask = sb("mask", [P, MSLOTS, NJ, CI], u8)
        xb = sb("xb", [P, XSLOTS, CH, F])
        S0 = sb("S0", [P, NJ, E0])
        Sw = sb("Sw", [P, NJ, H, 3, CF], bf16)
        Sv = sb("Sv", [P, NJ, H, 2, CF], fp16)
        Rb = sb("Rb", [P, H + 1, CI])
        adj_rows = sb("adj_rows", [P, ROWS, N], bf16)
        WT = [sb("WT0", [P, KC, E0]), sb("WT1", [P, KC, E1])]
        a_cols = sb("a_cols", [P, KC, 2 + 2 * H])
        b_col = sb("b_col", [P, KC])
        bias = sb("bias", [P, E1])
        ident = sb("ident", [P, P])
        identb = sb("identb", [P, P], bf16)
        mean_h = [sb("mean_h0", [P, E0]), sb("mean_h1", [P, E1])]
        ysum = sb("ysum", [P, 2, KC, NC])
        ysums = sb("ysums", [P, KC])
        stats = sb("stats", [P, 3, CH, 6])
        mv = sb("mv", [P, 3, CH, 2])
        var_eps = sb("var_eps", [P, 3, CH])
        neg_mean = sb("neg_mean", [P, 3, CH])
        half = sb("half", [P, CH])
        minus_half = sb("minus_half", [P, CH])
        minus_one = sb("minus_one", [P, CH])
        alone_now = sb("alone_now", [P, CH])
        rstd = sb("rstd", [P, 2, NC, CH])
        shift = sb("shift", [P, 2, NC, CH])
        w_norm = sb("w_norm", [P, KC])
        b_abs = sb("b_abs", [P, KC])
        f_bound = sb("f_bound", [P, KC])
        scale = sb("scale", [P, H])
        scale_inv = sb("scale_inv", [P, H])
        d_part = [sb("d_part0", [P, 1]), sb("d_part1", [P, H])]
        d_max = [sb("d_max0", [P, 1]), sb("d_max1", [P, H])]
        dd = [sb("dd0", [P, NJ, 1]), sb("dd1", [P, NJ, H])]
        ss = [sb("ss0", [P, NJ, 1]), sb("ss1", [P, NJ, H])]
        w = [sb("w0", [P, NJ, 1]), sb("w1", [P, NJ, H])]
        v = [sb("v0", [P, NJ, 1]), sb("v1", [P, NJ, H])]
        wv = sb("wv", [P, NJ, H])
        R = sb("R", [P, NJ, H + 1])
        Rs = sb("Rs", [P, NJ, H])
        R_now = sb("R_now", [P, CH, H + 1])
        alone = sb("alone", [P, NC, CH])
        denA = sb("denA", [P, CH])
        denB = sb("denB", [P, CH])

        accA = pb("accA", [P, CH, 512])
        accB = pb("accB", [P, 3, 512])
        misc_ps = pb("misc_ps", [P, 512])
        turn_ps = misc_ps[:, :].bitcast(bf16).rearrange("p (j i) -> p j i", j=8)
        S_AT = ((0, 0), (0, NS), (1, 0), (2, 0))
        N_AT = ((1, NS), (1, NS + NN), (2, NS), (2, NS + NN))

        def sums(kind, h):
            return accA if kind == "B" and h % 2 == 0 else accB

        names = """w_loaded consts prep_t prep_e bound setup x_loaded0 x_loaded1 x_loaded2 x_loaded3 adj0 adj1
            stats_done0 stats_done1 mv_ready0 mv_ready1 ve_ready0 ve_ready1 rstd_ready0 rstd_ready1
            norm_ready0 norm_ready1 y_ready yt_turned yt_ready feat_done feat_moved0 feat_moved1
            chain exp_ready scaled hv_ready ones_ready s_made s_chain n_made n_high n_rest sw_ready sv_ready
            misc_done misc_used tile_ready tile_free c_ready c0_ready n_ready bits_ready bits_free
            mask_turned mask_ready a_moved a_den a_rec a_sum x1_ready mean_added b_moved b_sum b_den x2_ready
            out_done r_now passed""".split()
        S = {n: sem(n) for n in names}
        x_loaded = [S[f"x_loaded{t}"] for t in range(NC)]
        adj_loaded = [S[f"adj{r}"] for r in range(ROWS)]

        def heads_view(L, col):
            if L == 0:
                return S0[:, :, F + col:F + col + 1]
            return S1.rearrange("p j (h e) -> p j h e", h=H)[:, :, :, C + col]

        def layer_index(ph, L):
            return 2 * ph if L == 0 else 2 * ph - 1

        def compares_before(kind, n):
            if kind == "B":
                first = NC * (B - 1)
                return [len(ab) * first + len(b) * (n - (NC + first))
                        for ab, b in zip(compared("AB"), compared("B"))]
            return [len(ab) * (n - NC) for ab in compared("AB")]

        def misc_before(kind, ph):
            first = 3 + NC
            each = 3 + (2 + H) + (H + 1) * NC
            return 0 if kind == "A" else each * ph + (first - each)

        def misc_before_layer(kind, ph, L):
            return misc_before(kind, ph) + (2 + H if L == 0 and kind != "A" else 0)

        def misc_before_step(kind, ph, c):
            if kind == "A":
                return 3 + c
            if kind == "B":
                return misc_before(kind, ph) + (2 + H) + H * c
            return misc_before(kind, ph) + (5 + H) + (H + 1) * c

        def turned_before(kind, ph):
            return {"A": 0, "AB": 2 * CH * NC * ph + 2 * CH, "B": 2 * CH * CHUNKS}[kind]

        def r_now_before(kind, ph):
            return 0 if kind == "A" else (NC + 2) * ph + (NC + 1 - (NC + 2))

        def rb_for(kind, ph, c, unit):
            if kind == "A":
                return 3 + c
            if kind == "B":
                return misc_before(kind, ph) + H * c + (3 + unit)
            place = {H: H - 1, H - 1: H}.get(unit, unit)
            return misc_before(kind, ph) + (H + 1) * c + (5 + place)

        def wait(eng, s, value):
            if not isinstance(value, int) or value > 0:
                eng.wait_ge(s, value)

        def wait_alone(eng, s, value):
            wait(eng, s, value)
            eng.sem_inc(S["passed"], 1)

        def phases(eng, features, steps, first_chunk=lambda: None):
            features("A", 0)
            first_chunk()
            steps("A", STEP_A_FIRST, 0, 0)
            with eng.Fori(1, NC) as c:
                steps("A", STEP_A, 0, c)
            steps("A", STEP_A_END, 0, NC - 1)
            with eng.Fori(1, B - 1) as ph:
                features("AB", ph)
                with eng.Fori(0, NC - 1) as c:
                    steps("AB", STEP_AB, ph, c)
                steps("AB", STEP_AB, ph, NC - 1)
            features("AB", B - 1)
            with eng.Fori(0, NC - 2) as c:
                steps("AB", STEP_AB, B - 1, c)
            steps("AB", STEP_AB_NEXT_LAST, B - 1, NC - 2)
            steps("AB", STEP_AB_LAST, B - 1, NC - 1)
            features("B", B)
            with eng.Fori(0, NC) as c:
                steps("B", STEP_B, B, c)

        block = ctx.enter_context(nc.Block())

        @block.sync
        def _(sp):
            def load_x(m, t):
                return sp.dma_start(xb[:, m % XSLOTS, :, :],
                                    x_rows[m, :, :, :]).then_inc(x_loaded[t], 16)

            x_rows = x_in.rearrange("b (c k p) f -> (b c) p k f", k=CH, p=P)
            out_rows = out.rearrange("b (c k p) f -> (b c) p k f", k=CH, p=P)
            for L, Wd in enumerate((W0, W1)):
                sp.dma_start(Wn[:, L, :, :], Wd.rearrange("(k p) f -> p k f", p=P)).then_inc(S["w_loaded"], 16)
            sp.wait_ge(S["consts"], 1)
            with nc.allow_non_contiguous_dma("small vectors, once"):
                for col, a in enumerate((a0_dst, a0_src)):
                    sp.dma_start(a_cols[:, :, col], a.rearrange("(k p) -> p k", p=P)).then_inc(S["w_loaded"], 16)
                sp.dma_start(b_col[:, :], b1.rearrange("(k p) -> p k", p=P)).then_inc(S["w_loaded"], 16)
                for h in range(H):
                    p0, k = h * C % P, h * C // P
                    for which in range(2):
                        sp.dma_start(a_cols[p0:p0 + C, k, 2 + 2 * h + which],
                                     a1[h, (1 - which) * C:(2 - which) * C]).then_inc(S["w_loaded"], 16)
            sp.dma_start(bias[:, :].rearrange("p (h e) -> p h e", h=H)[:, :, 0:C],
                         b1.rearrange("(h c) -> h c", h=H).partition_broadcast(P)).then_inc(S["w_loaded"], 16)
            for m in range(XSLOTS):
                if m >= NC:
                    sp.wait_ge(x_loaded[m - NC], 16)
                load_x(m, m % NC)

            def store(m):
                sp.wait_ge(S["x2_ready"], H * m + (H + 1))
                sp.dma_start(out_rows[m, :, :, :], xb[:, m % XSLOTS, :, :]).then_inc(S["out_done"], 16)
                wait_alone(sp, S["out_done"], 16 * m + 16)

            with sp.Fori(0, B - 2) as b:
                for t in range(NC):
                    store(NC * b + t)
                    load_x(NC * b + (t + XSLOTS), t)
            with sp.Fori(NC * (B - 2), CHUNKS) as m:
                store(m)

        @block.gpsimd
        def _(pool):
            adj_view = adj.rearrange("b (q r p) n -> (b q) r p n", r=CH, p=P)

            def load_adj(q, r):
                wait(pool, S["mask_turned"], 2 * CH * q + 2 * (r - ROWS + 1))
                pool.dma_start(adj_rows[:, r % ROWS, :], adj_view[q, r, :, :]).then_inc(adj_loaded[r % ROWS], 16)

            pool.sem_inc(S["x1_ready"], 1)
            pool.sem_inc(S["norm_ready1"], 1)
            pool.sem_inc(S["x2_ready"], 1)
            pool.memset(a_cols[:, :, :], 0.0).then_inc(S["consts"], 1)
            for r in range(ROWS):
                load_adj(0, r)
            pool.memset(half[:, :], 0.5)
            pool.memset(minus_half[:, :], -0.5)
            pool.memset(minus_one[:, :], -1.0)
            pool.memset(R[:, :, :], 0.0)
            for t in (ident, identb):
                last = pool.memset(t[:, :], 0.0)
            last.then_inc(S["consts"], 1)
            pool.wait_ge(S["consts"], 2)
            for t in (ident, identb):
                last = pool.affine_select(out=t[:, :], in_=t[:, :], compare_op=ALU.not_equal, fill=1.0, base=0,
                                          pattern=[[-1, P]], channel_multiplier=1)
            last.then_inc(S["consts"], 1)
            pool.wait_ge(S["bound"], 1)
            pool.tensor_tensor(w_norm[:, :], w_norm[:, :], half[:, 0:KC], ALU.pow).then_inc(S["bound"], 1)
            pool.wait_ge(S["bound"], 4)
            pool.tensor_tensor(scale[:, :], scale_inv[:, :], minus_one[:, 0:H], ALU.pow).then_inc(S["bound"], 1)

            def norm(L, n, slot, place):
                mv_ready, ve_ready = S[f"mv_ready{L}"], S[f"ve_ready{L}"]
                rstd_ready, norm_ready = S[f"rstd_ready{L}"], S[f"norm_ready{L}"]
                if L == 0:
                    wait_alone(pool, norm_ready, n - 1)
                wait_alone(pool, mv_ready, n + 1)
                pool.tensor_scalar(var_eps[:, slot, :], mv[:, slot, :, 1], EPS, None, ALU.add)
                pool.tensor_scalar(neg_mean[:, slot, :], mv[:, slot, :, 0], -1.0, None, ALU.mult)\
                    .then_inc(ve_ready, 1)
                pool.wait_ge(ve_ready, n + 1)
                pool.tensor_tensor(rstd[:, L, place, :], var_eps[:, slot, :], minus_half[:, :], ALU.pow)\
                    .then_inc(rstd_ready, 1)
                pool.wait_ge(rstd_ready, n + 1)
                pool.tensor_tensor(shift[:, L, place, :], rstd[:, L, place, :], neg_mean[:, slot, :], ALU.mult)\
                    .then_inc(norm_ready, 1)

            def features(kind, ph):
                if kind == "A":
                    for t in range(NC):
                        norm(0, t, t % 2, t)
                    return
                if kind == "AB":
                    for t in range(NC):
                        norm(0, NC * ph + t, t % 2, t)
                wait_alone(pool, S["exp_ready"], 4 * ph)
                pool.tensor_tensor(v[1][:, :, :], v[1][:, :, :],
                                   scale[:, :].unsqueeze(1).to_broadcast([P, NJ, H]), ALU.mult)
                pool.tensor_tensor(Rs[:, :, :], R[:, :, 0:H],
                                   scale_inv[:, :].unsqueeze(1).to_broadcast([P, NJ, H]), ALU.mult)\
                    .then_inc(S["scaled"], 1)
                wait_alone(pool, S["scaled"], ph)

                def raw_of(t):
                    return S1[:, CH * t:CH * t + CH, :].rearrange("p j (h e) -> p (j h) e", h=H)[:, :, 0:CF]

                def rest(t):
                    high = Sv[:, CH * t:CH * t + CH, :, 0, :].rearrange("p j h e -> p (j h) e")
                    wait_alone(pool, S["n_high"], NC * (ph - 1) + (t + 1))
                    pool.tensor_tensor(raw_of(t), raw_of(t), high, ALU.subtract).then_inc(S["n_rest"], 1)

                for t in range(NC):
                    wait_alone(pool, S["s_made"], NC * (ph - 1) + (t + 1))
                    vs = v[1][:, CH * t:CH * t + CH, :].rearrange("p j h -> p (j h)").unsqueeze(2)
                    pool.tensor_tensor(raw_of(t), raw_of(t), vs.to_broadcast([P, CH * H, CF]), ALU.mult)\
                        .then_inc(S["n_made"], 1)
                    if t:
                        rest(t - 1)
                rest(NC - 1)

            def steps(kind, events, ph, c):
                n = ph * NC + c
                for e in events:
                    if e[0] == "X1":
                        norm(1, n - e[1], 2, c - e[1])
                    elif e[0] == "EB":
                        h = e[1]
                        g = H * (n - NC) + h
                        xs = xb[:, (n + NC) % XSLOTS, :, h * C:(h + 1) * C]
                        ns, nn = numS[:, :, 0:CF], numN[:, :, 0:CF]

                        def done(i):
                            wait_alone(pool, S["b_sum"], 6 * g + (i + 1))

                        wait_alone(pool, S["b_moved"], g + 2)
                        if h == 0:
                            wait_alone(pool, S["mean_added"], n - (NC - 1))
                        low = numN[:, :, CF:2 * CF]
                        pool.tensor_scalar(low, low, 1 / LOW, None, ALU.mult)
                        pool.tensor_tensor(ns, ns, numS[:, :, CF:2 * CF], ALU.add).then_inc(S["b_sum"], 1)
                        done(0)
                        pool.tensor_tensor(nn, nn, low, ALU.add)
                        pool.tensor_tensor(ns, ns, numS[:, :, 2 * CF:3 * CF], ALU.add).then_inc(S["b_sum"], 1)
                        done(1)
                        r_rows = Rs[:, :, :].rearrange("p (c k) h -> p c k h", k=CH)[:, c, :, h:h + 1]
                        pool.tensor_tensor(nn, nn, r_rows.to_broadcast([P, CH, CF]), ALU.mult)\
                            .then_inc(S["b_sum"], 1)
                        done(2)
                        pool.tensor_tensor(ns, ns, nn, ALU.add).then_inc(S["b_sum"], 1)
                        done(3)
                        pool.tensor_scalar(denB[:, :], ns[:, :, C], TINY, None, ALU.max).then_inc(S["b_sum"], 1)
                        done(4)
                        pool.tensor_tensor(denB[:, :], denB[:, :], minus_one[:, :], ALU.pow)\
                            .then_inc(S["b_sum"], 1)
                        done(5)
                        pool.tensor_tensor(ns[:, :, 0:C], ns[:, :, 0:C],
                                           denB[:, :].unsqueeze(2).to_broadcast([P, CH, C]), ALU.mult)\
                            .then_inc(S["b_den"], 1)
                        wait_alone(pool, S["b_den"], g + 1)
                        pool.tensor_tensor(xs, xs, ns[:, :, 0:C], ALU.add).then_inc(S["x2_ready"], 1)
                    elif e[0] == "L":
                        load_adj(n + e[1], e[2])

            def first_chunk():
                for r in range(ROWS, CH):
                    load_adj(0, r)
                for r in range(ROWS):
                    load_adj(1, r)

            phases(pool, features, steps, first_chunk)

        @block.scalar
        def _(act):
            act.sem_inc(S["a_moved"], 1)
            act.sem_inc(S["b_moved"], 1)
            for L in range(2):
                for k in range(KC):
                    i = 2 * (KC * L + k)
                    act.wait_ge(S["prep_t"], i + 1)
                    src = accA[:, 0, 0:F]
                    if L == 0:
                        nc.scalar.activation(WT[0][:, k, 0:F], src, ACT.Copy).then_inc(S["prep_e"], 1)
                    else:
                        nc.scalar.activation(WT[1][:, k, :].rearrange("p (h e) -> p h e", h=H)[:, :, 0:C],
                                             src.rearrange("p (h c) -> p h c", h=H), ACT.Copy)\
                            .then_inc(S["prep_e"], 1)
                    act.wait_ge(S["prep_t"], i + 2)
                    if L == 0:
                        nc.scalar.activation(WT[0][:, k, F:F + 2], accA[:, 1, 0:2], ACT.Copy)\
                            .then_inc(S["prep_e"], 1)
                    else:
                        nc.scalar.activation(WT[1][:, k, :].rearrange("p (h e) -> p h e", h=H)[:, :, C:C + 2],
                                             accA[:, 1, 0:2 * H].rearrange("p (h e) -> p h e", h=H), ACT.Copy)\
                            .then_inc(S["prep_e"], 1)
            act.wait_ge(S["prep_t"], 4 * KC + 1)
            nc.scalar.activation(bias[:, :].rearrange("p (h e) -> p h e", h=H)[:, :, C:C + 2],
                                 accA[:, 2, 0:2 * H].rearrange("p (h e) -> p h e", h=H), ACT.Copy)\
                .then_inc(S["prep_e"], 1)

            def move_mask(q, r, half_):
                act.wait_ge(S["mask_turned"], 2 * CH * q + (2 * r + half_ + 1))
                nc.scalar.activation(mask[:, q % MSLOTS, 8 * half_:8 * half_ + 8, r * P:(r + 1) * P],
                                     turn_ps[:, :, :], ACT.Copy, scale=MARK).then_inc(S["mask_ready"], 1)

            def move_rb(misc, unit):
                act.wait_ge(S["misc_done"], misc + 1)
                nc.scalar.activation(Rb[:, unit, :], misc_ps[:, :], ACT.Copy).then_inc(S["misc_used"], 1)

            def norm(ph, L, t, ks=range(CH)):
                f, s = NC * layer_index(ph, L) + t, t % 2
                wait(act, S["yt_turned"], f - 1)
                wait_alone(act, S[f"norm_ready{L}"], NC * (ph - L) + (t + 1 + L))
                for k in ks:
                    nc.scalar.activation(y[:, s, k, :], xb[:, (NC * (ph - L) + t) % XSLOTS, k, :], ACT.Relu,
                                         bias=shift[:, L, t, k:k + 1], scale=rstd[:, L, t, k:k + 1])\
                        .then_inc(S["y_ready"], 1)

            def features(kind, ph):
                def move_yt(L, t):
                    f, s = NC * layer_index(ph, L) + t, t % 2
                    act.wait_ge(S["yt_turned"], f + 1)
                    wait(act, S["feat_done"], CH * (f - 1))
                    for k in range(KC):
                        nc.scalar.activation(yT[:, s, k, :], accA[:, k, :], ACT.Copy,
                                             accum_out=ysum[:, L, k, t:t + 1]).then_inc(S["yt_ready"], 1)

                def move_features(t, ks):
                    for k in ks:
                        act.wait_ge(S["feat_done"], CH * (NC * layer_index(ph, 0) + t) + (k + 1))
                        nc.scalar.activation(S0[:, CH * t + k, :], accA[:, 2 + k % 2, 0:E0], ACT.Copy)\
                            .then_inc(S["feat_moved0"], 1)

                def exps(L):
                    i = layer_index(ph, L)
                    act.wait_ge(S["chain"], 4 * i + 4)
                    nc.scalar.activation(v[L][:, :, :], dd[L][:, :, :], ACT.Exp, scale=LEAKY)\
                        .then_inc(S["exp_ready"], 1)
                    if L == 1:
                        nc.scalar.activation(wv[:, :, :], dd[1][:, :, :], ACT.Exp)
                    nc.scalar.activation(w[L][:, :, :], dd[L][:, :, :], ACT.Exp, scale=1 - LEAKY)
                    col = slice(H, H + 1) if L == 0 else slice(0, H)
                    nc.scalar.activation(R[:, :, col], ss[L][:, :, :], ACT.Exp, scale=-(1 - LEAKY))\
                        .then_inc(S["exp_ready"], 1)
                    act.wait_ge(S["exp_ready"], 2 * i + 2)
                    nc.scalar.activation(R_now[:, :, col], R[:, 0:CH, col], ACT.Copy).then_inc(S["r_now"], 1)

                def scale_features(t):
                    for j in range(CH * t, CH * t + CH):
                        nc.scalar.activation(S0[:, j, 0:F], S0[:, j, 0:F], ACT.Copy, scale=v[0][:, j, :])
                    js = slice(CH * t, CH * t + CH)
                    nc.scalar.activation(S0[:, js, F:F + 1], v[0][:, js, :], ACT.Copy).then_inc(S["hv_ready"], 1)

                def low(t):
                    act.wait_ge(S["n_rest"], NC * (ph - 1) + (t + 1))
                    nc.scalar.activation(Sv[:, CH * t:CH * t + CH, :, 1, :].rearrange("p j h e -> p (j h) e"),
                                         S1[:, CH * t:CH * t + CH, :]
                                         .rearrange("p j (h e) -> p (j h) e", h=H)[:, :, 0:CF],
                                         ACT.Copy, scale=LOW).then_inc(S["sv_ready"], 1)

                m1, m0 = misc_before_layer(kind, ph, 1) + 2, misc_before_layer(kind, ph, 0) + 2
                if kind != "A":
                    move_yt(1, 0)
                    wait(act, S["x1_ready"], NC * ph + 1)
                    norm(ph, 1, 1)
                    for t in range(1, NC):
                        move_yt(1, t)
                        if t + 1 < NC:
                            norm(ph, 1, t + 1)
                        elif kind == "AB":
                            norm(ph, 0, 0)
                if kind == "A":
                    norm(ph, 0, 0)
                if kind == "B":
                    exps(1)
                    for unit in range(H):
                        move_rb(m1 + unit, unit)
                    for t in range(NC):
                        low(t)
                    return
                both = kind == "AB"
                move_yt(0, 0)
                norm(ph, 0, 1)
                if both:
                    exps(1)
                for t in range(NC):
                    if t + 1 < NC:
                        move_yt(0, t + 1)
                    if both and t in (1, 2):
                        move_rb(m1 + (2 * t - 2), 2 * t - 2)
                    move_features(t, [0])
                    if t + 2 < NC:
                        norm(ph, 0, t + 2, [0, 1])
                    move_features(t, [1])
                    if t + 2 < NC:
                        norm(ph, 0, t + 2, [2, 3])
                    move_features(t, [2, 3])
                    if both and t in (1, 2):
                        move_rb(m1 + (2 * t - 1), 2 * t - 1)
                    if both and t >= 2:
                        low(t - 2)
                exps(0)
                scale_features(0)
                move_rb(m0, H)
                for t in range(1, NC):
                    scale_features(t)
                    if both and t == 1:
                        low(NC - 2)
                        low(NC - 1)

            def steps(kind, events, ph, c):
                n = ph * NC + c
                misc = misc_before_step(kind, ph, c)
                first_r = True

                def compare(i):
                    h, g, place = i // G, i % G, mine.index(i)
                    slot = place % CRING
                    if first_of[h] == i:
                        act.wait_ge(S["misc_used"], rb_for(kind, ph, c, h))
                    used = mine[place - CRING] if place >= CRING else mine[place - CRING] - HG
                    act.wait_ge(S["n_ready"], HG * (n - NC) + (NR + used + 1))
                    for jj in range(JG):
                        last = nc.scalar.activation(cmp[:, slot, jj, :], Rb[:, h, :], ACT.Sign,
                                                    bias=w[1][:, JG * g + jj, h:h + 1], scale=-1.0)
                    last.then_inc(S["c_ready"], 1)

                mine = compared(kind)[1]
                before = compares_before(kind, n)
                first_of = [min(i for i in mine if i // G == h) for h in range(H)]
                ahead, nxt = {}, mine[0] + 1
                for e in events:
                    if e[0] == "G":
                        i = G * e[1] + e[2]
                        upto = min(i + (LEAD - 1 if i < G else LEAD), HG - 1)
                        ahead[i] = [i2 for i2 in range(nxt, upto + 1) if i2 in mine]
                        nxt = max(nxt, upto + 1)
                if kind != "A":
                    compare(mine[0])
                for e in events:
                    if e[0] == "M":
                        move_mask(n + 1, e[1], e[2])
                    elif e[0] == "R":
                        if first_r:
                            R_chunks = R[:, :, :].rearrange("p (c k) u -> p c k u", k=CH)
                            nc.scalar.activation(R_now[:, :, :], R_chunks[:, (c + 1) % NC, :, :],
                                                 ACT.Copy).then_inc(S["r_now"], 1)
                            first_r = False
                        if e[1] == H:
                            act.wait_ge(S["tile_ready"], NJ * n + NJ)
                        else:
                            own, theirs = [sum(i < G * e[1] + G for i in part_) for part_ in compared(kind)[::-1]]
                            act.wait_ge(S["c_ready"], before[1] + own)
                            act.wait_ge(S["c0_ready"], before[0] + theirs)
                        move_rb(misc, e[1])
                        misc = misc + 1
                    elif e[0] == "G":
                        for i in ahead[G * e[1] + e[2]]:
                            compare(i)
                    elif e[0] == "EA":
                        act.wait_ge(S["tile_free"], NJ * n + (RING + NJ))
                        act.wait_ge(S["x1_ready"], n + 1)
                        nc.scalar.activation(numA[:, :, :], accA[:, :, 0:F + 1], ACT.Copy)\
                            .then_inc(S["a_moved"], 1)
                    elif e[0] == "X1" and isinstance(c, int) and c == NC - 1:
                        if kind != "A":
                            act.wait_ge(S["n_ready"], HG * (n - NC) + (NR + HG))
                        norm(ph + 1, 1, 0)
                    elif e[0] == "EB":
                        h = e[1]
                        acc = sums(kind, h)
                        act.wait_ge(S["bits_free"], HG * (n - NC) + (BRING + G * h + G))
                        act.wait_ge(S["x2_ready"], H * (n - NC) + (h + 1))
                        nc.scalar.activation(numS[:, 0:2, :].rearrange("p k e -> p (k e)"), acc[:, 0, 0:2 * NS],
                                             ACT.Copy)
                        nc.scalar.activation(numS[:, 2:4, :], acc[:, 1:3, 0:NS], ACT.Copy)
                        nc.scalar.activation(numN.rearrange("p (b k) e -> p b (k e)", b=2),
                                             acc[:, 1:3, NS:NS + 2 * NN], ACT.Copy).then_inc(S["b_moved"], 1)

            def first_chunk():
                for r in range(CH):
                    for half_ in range(2):
                        move_mask(0, r, half_)

            phases(act, features, steps, first_chunk)

        @block.tensor
        def _(pe):
            pe.wait_ge(S["consts"], 3)
            pe.wait_ge(S["w_loaded"], 16 * (6 + 2 * H))
            for L in range(2):
                acols = a_cols[:, :, 0:2] if L == 0 else a_cols[:, :, 2:2 + 2 * H]
                na = 2 * HEADS[L]
                for k in range(KC):
                    i = 2 * (KC * L + k)
                    wait(pe, S["prep_e"], i)
                    for o in range(KC):
                        last = nc.tensor.transpose(accA[:, 0, o * P:(o + 1) * P],
                                                   Wn[:, L, o, k * P:(k + 1) * P], ident[:, :])
                    last.then_inc(S["prep_t"], 1)
                    for o in range(KC):
                        last = nc.tensor.matmul(accA[:, 1, 0:na], Wn[:, L, o, k * P:(k + 1) * P],
                                                acols[:, o, :], start=o == 0, stop=o == KC - 1)
                    last.then_inc(S["prep_t"], 1)
            for o in range(KC):
                last = nc.tensor.matmul(accA[:, 2, 0:2 * H], b_col[:, o:o + 1].to_broadcast([P, P]),
                                        a_cols[:, o, 2:2 + 2 * H], start=o == 0, stop=o == KC - 1)
            last.then_inc(S["prep_t"], 1)
            pe.wait_ge(S["bound"], 3)
            for o in range(KC):
                last = nc.tensor.transpose(accA[:, 3, o * P:(o + 1) * P],
                                           f_bound[:, o:o + 1].to_broadcast([P, P]), ident[:, :])
            last.then_inc(S["prep_t"], 1)
            pe.wait_ge(S["prep_e"], 4 * KC + 1)

            def turn_mask(q, r, half_, misc):
                if half_ == 0:
                    pe.wait_ge(adj_loaded[r % ROWS], 16 * (CH // ROWS) * q + 16 * (r // ROWS + 1))
                wait(pe, S["mask_ready"], 2 * CH * q + (2 * r + half_))
                wait(pe, S["misc_used"], misc)
                for j in range(8):
                    col = (8 * half_ + j) * P
                    last = nc.tensor.transpose(turn_ps[:, j, :], adj_rows[:, r % ROWS, col:col + P], identb[:, :])
                last.then_inc(S["mask_turned"], 1)

            def turn_r(misc, unit, turned):
                wait(pe, S["misc_used"], misc)
                wait(pe, S["mask_ready"], turned)
                for k in range(CH):
                    last = nc.tensor.transpose(misc_ps[:, k * P:(k + 1) * P],
                                               R_now[:, k, unit:unit + 1].to_broadcast([P, P]), ident[:, :])
                last.then_inc(S["misc_done"], 1)

            def features(kind, ph):
                def turn_y(L, t):
                    f, s = NC * layer_index(ph, L) + t, t % 2
                    wait(pe, S["yt_ready"], 2 * f)
                    for k in range(CH):
                        pe.wait_ge(S["y_ready"], CH * f + (k + 1))
                        for kc in range(KC):
                            last = nc.tensor.transpose(accA[:, kc, k * P:(k + 1) * P],
                                                       y[:, s, k, kc * P:(kc + 1) * P], ident[:, :])
                    last.then_inc(S["yt_turned"], 1)

                def feats(L, t):
                    f, s = NC * layer_index(ph, L) + t, t % 2
                    pe.wait_ge(S["yt_ready"], 2 * f + 2)
                    for k in range(CH):
                        if L == 0 and kind == "AB" and CH * t + k < 2:
                            pe.wait_ge(S["feat_moved1"], CH * NC * ph + (k - 1))
                        elif CH * t + k >= 2:
                            pe.wait_ge(S[f"feat_moved{L}"], CH * NC * (ph - L) + (CH * t + k - 1))
                        for kc in range(KC):
                            last = nc.tensor.matmul(accA[:, 2 + k % 2, 0:COLS[L]], yT[:, s, kc, k * P:(k + 1) * P],
                                                    WT[L][:, kc, :], start=kc == 0, stop=kc == KC - 1)
                        last.then_inc(S["feat_done"], 1)

                def turn_max(L):
                    i, m = layer_index(ph, L), misc_before_layer(kind, ph, L)
                    pe.wait_ge(S["chain"], 4 * i + 1)
                    wait(pe, S["misc_used"], m)
                    wait(pe, S["mask_ready"], turned_before(kind, ph))
                    for h in range(HEADS[L]):
                        last = nc.tensor.transpose(misc_ps[:, h * P:(h + 1) * P],
                                                   d_part[L][:, h:h + 1].to_broadcast([P, P]), ident[:, :])
                    last.then_inc(S["misc_done"], 1)

                def mean(L):
                    i, m = layer_index(ph, L), misc_before_layer(kind, ph, L)
                    pe.wait_ge(S["chain"], 4 * i + 2)
                    pe.wait_ge(S["misc_used"], m + 1)
                    for kc in range(KC):
                        last = nc.tensor.matmul(misc_ps[:, 0:COLS[L]], ysums[:, kc:kc + 1].to_broadcast([P, P]),
                                                WT[L][:, kc, :], start=kc == 0, stop=kc == KC - 1)
                    last.then_inc(S["misc_done"], 1)

                def first_r(L, units):
                    pe.wait_ge(S["r_now"], r_now_before(kind, ph) + (1 if L == 1 or kind == "A" else 2))
                    for unit in units:
                        turn_r(misc_before_layer(kind, ph, L) + (2 + (unit if L == 1 else 0)), unit, 0)

                if kind != "A":
                    pe.wait_ge(S["a_moved"], ph * NC + 1)
                    turn_y(1, 0)
                    for t in range(NC):
                        if t + 1 < NC:
                            turn_y(1, t + 1)
                        feats(1, t)
                if kind == "B":
                    turn_max(1)
                    mean(1)
                    first_r(1, range(H))
                    return
                both = kind == "AB"
                turn_y(0, 0)
                if both:
                    turn_max(1)
                turn_y(0, 1)
                if both:
                    mean(1)
                feats(0, 0)
                for t in range(1, NC):
                    if t + 1 < NC:
                        turn_y(0, t + 1)
                    if both and t in (1, 2):
                        first_r(1, [2 * t - 2])
                    feats(0, t)
                    if both and t in (1, 2):
                        first_r(1, [2 * t - 1])
                turn_max(0)
                mean(0)
                first_r(0, (H,))

            def steps(kind, events, ph, c):
                n = ph * NC + c
                misc = misc_before_step(kind, ph, c)
                turned = 2 * CH * CHUNKS if kind == "B" else 2 * CH * n + 2 * CH
                first_r = True
                for e in events:
                    if e[0] == "A":
                        j = e[1]
                        if j == 0:
                            pe.wait_ge(S["a_moved"], n + 1)
                        if j % CH == 0:
                            t = j // CH
                            wait_alone(pe, S["hv_ready"], NC * ph + (t + 1))
                        pe.wait_ge(S["tile_ready"], NJ * n + (j + 1))
                        for k in range(CH):
                            last = nc.tensor.matmul(accA[:, k, 0:F + 1], tiles[:, j % RING, k * P:(k + 1) * P],
                                                    S0[:, j, 0:F + 1], start=j == 0, stop=j == NJ - 1)
                        last.then_inc(S["tile_free"], 1)
                    elif e[0] == "G":
                        h, g = e[1:]
                        acc = sums(kind, h)
                        if h == 0:
                            wait_alone(pe, S["sw_ready"], NC * (ph - 1) + (g + 1))
                            wait_alone(pe, S["sv_ready"], NC * (ph - 1) + (g + 1))
                        if g == 0:
                            pe.wait_ge(S["b_moved"], H * (n - NC) + (h if kind == "B" else h + 1))
                        wait_alone(pe, S["bits_ready"], HG * (n - NC) + (G * h + g + 1))
                        for jj in range(JG):
                            j = JG * g + jj
                            for k in range(CH):
                                bank, col = S_AT[k]
                                nc.tensor.matmul(acc[:, bank, col:col + NS],
                                                 bits[:, g % BRING, 1, jj, k * P:(k + 1) * P],
                                                 Sw[:, j, h, :, :].rearrange("p a e -> p (a e)"),
                                                 start=j == 0 and col == 0, stop=j == NJ - 1, skip_group_check=True)
                            for k in range(CH):
                                bank, col = N_AT[k]
                                last = nc.tensor.matmul(acc[:, bank, col:col + NN],
                                                        bits[:, g % BRING, 0, jj, k * P:(k + 1) * P],
                                                        Sv[:, j, h, :, :].rearrange("p a e -> p (a e)"),
                                                        start=False, stop=j == NJ - 1, skip_group_check=True)
                        last.then_inc(S["bits_free"], 1)
                    elif e[0] == "M":
                        turn_mask(n + 1, e[1], e[2], misc)
                        turned = turned + 1
                    elif e[0] == "R":
                        if first_r:
                            pe.wait_ge(S["r_now"], r_now_before(kind, ph) + c + (3 if kind == "AB" else 2))
                            first_r = False
                        turn_r(misc, e[1], turned)
                        misc = misc + 1

            def first_chunk():
                for r in range(CH):
                    for half_ in range(2):
                        turn_mask(0, r, half_, 3)

            phases(pe, features, steps, first_chunk)

        @block.vector
        def _(dve):
            dve.sem_inc(S["tile_free"], RING)
            dve.sem_inc(S["bits_free"], BRING)
            dve.sem_inc(S["n_ready"], NR)
            dve.wait_ge(S["w_loaded"], 16 * (6 + 2 * H))
            nc.vector.tensor_tensor(squares, Wn[:, 1, :, :], Wn[:, 1, :, :], ALU.mult).then_inc(S["setup"], 1)
            nc.vector.scalar_tensor_tensor(out=b_abs[:, :], in0=b_col[:, :], scalar=-1.0, in1=b_col[:, :],
                                           op0=ALU.mult, op1=ALU.max).then_inc(S["setup"], 1)
            dve.wait_ge(S["setup"], 2)
            nc.vector.tensor_reduce(w_norm[:, :], squares, AX.X, ALU.add).then_inc(S["bound"], 1)
            dve.wait_ge(S["bound"], 2)
            nc.vector.scalar_tensor_tensor(out=f_bound[:, :], in0=w_norm[:, :], scalar=float(F) ** 0.5,
                                           in1=b_abs[:, :], op0=ALU.mult, op1=ALU.add).then_inc(S["bound"], 1)
            dve.wait_ge(S["prep_t"], 4 * KC + 2)
            nc.vector.tensor_reduce(scale_inv[:, :], accA[:, 3, 0:F].rearrange("p (h c) -> p h c", h=H),
                                    AX.X, ALU.max).then_inc(S["setup"], 1)
            dve.wait_ge(S["setup"], 3)
            nc.vector.tensor_scalar(scale_inv[:, :], scale_inv[:, :], 1.0, 2.0 ** -14, ALU.max, ALU.mult)\
                .then_inc(S["bound"], 1)

            def mean_variance(L, n, slot, used):
                wait_alone(dve, S[f"norm_ready{L}"], used)
                for k in range(CH):
                    last = nc.vector.bn_stats(stats[:, slot, k, :], xb[:, n % XSLOTS, k, :])
                last.then_inc(S[f"stats_done{L}"], 1)
                wait_alone(dve, S[f"stats_done{L}"], n + 1)
                for k in range(CH):
                    last = nc.vector.bn_aggr(mv[:, slot, k, :], stats[:, slot, k, :])
                last.then_inc(S[f"mv_ready{L}"], 1)

            def features(kind, ph):
                def statistics0(t):
                    dve.wait_ge(x_loaded[t], 16 * ph + 16)
                    mean_variance(0, NC * ph + t, t % 2, NC * ph + t - 1)

                def move_features(t):
                    for k in range(CH):
                        g = CH * (NC * layer_index(ph, 1) + t) + k
                        dve.wait_ge(S["feat_done"], g + 1)
                        nc.vector.tensor_tensor(S1[:, CH * t + k, :], accA[:, 2 + k % 2, 0:E1], bias[:, :], ALU.add)\
                            .then_inc(S["feat_moved1"], 1)

                def maxima(L):
                    first = NC * layer_index(ph, L)
                    dve.wait_ge(S[f"feat_moved{L}"], CH * NC * (ph - L + 1))
                    nc.vector.tensor_reduce(d_part[L][:, :], heads_view(L, 0).rearrange("p j h -> p h j"),
                                            AX.X, ALU.max).then_inc(S["chain"], 1)
                    dve.wait_ge(S["yt_ready"], 2 * (first + NC))
                    if L == 0 and kind == "AB":
                        dve.wait_ge(S["misc_done"], misc_before_layer(kind, ph, 1) + 2)
                    nc.vector.tensor_reduce(ysums[:, :], ysum[:, L, :, :], AX.X, ALU.add).then_inc(S["chain"], 1)

                def shifted(L):
                    i, m, nh = layer_index(ph, L), misc_before_layer(kind, ph, L), HEADS[L]
                    dve.wait_ge(S["misc_done"], m + 1)
                    nc.vector.tensor_reduce(d_max[L][:, :], misc_ps[:, 0:nh * P].rearrange("p (h n) -> p h n", h=nh),
                                            AX.X, ALU.max).then_inc(S["misc_used"], 1)
                    dve.wait_ge(S["misc_used"], m + 1)
                    dmax_b = d_max[L][:, :].unsqueeze(1).to_broadcast([P, NJ, nh])
                    nc.vector.tensor_tensor(dd[L][:, :, :], heads_view(L, 0), dmax_b, ALU.subtract)
                    nc.vector.tensor_tensor(ss[L][:, :, :], heads_view(L, 1), dmax_b, ALU.add).then_inc(S["chain"], 1)
                    dve.wait_ge(S["chain"], 4 * i + 3)
                    nc.vector.tensor_scalar(ss[L][:, :, :], ss[L][:, :, :], 0.0, None, ALU.max)\
                        .then_inc(S["chain"], 1)
                    if L == 1:
                        nc.vector.memset(heads_view(1, 0), 1.0).then_inc(S["ones_ready"], 1)

                def mean(L):
                    m = misc_before_layer(kind, ph, L)
                    dve.wait_ge(S["misc_done"], m + 2)
                    if L == 0:
                        nc.vector.tensor_scalar(mean_h[0][:, :], misc_ps[:, 0:E0], 1.0 / N, None, ALU.mult)\
                            .then_inc(S["misc_used"], 1)
                    else:
                        nc.vector.scalar_tensor_tensor(out=mean_h[1][:, :], in0=misc_ps[:, 0:E1], scalar=1.0 / N,
                                                       in1=bias[:, :], op0=ALU.mult, op1=ALU.add)\
                            .then_inc(S["misc_used"], 1)

                def split_features(t, halves=(0, 1)):
                    js = slice(CH * t, CH * t + CH)
                    i = NC * (ph - 1) + t
                    raw = S1[:, js, :].rearrange("p j (h e) -> p (j h) e", h=H)[:, :, 0:CF]
                    parts = Sw[:, js, :, :, :].rearrange("p j h a e -> p (j h) a e")
                    if 0 in halves:
                        if t == 0:
                            dve.wait_ge(S["ones_ready"], ph)
                            dve.wait_ge(S["exp_ready"], 4 * ph)
                            dve.wait_ge(S["x2_ready"], H * NC * (ph - 1) + 1)
                        else:
                            dve.wait_ge(S["sw_ready"], i)
                        ws = wv[:, js, :].rearrange("p j h -> p (j h)").unsqueeze(2)
                        nc.vector.tensor_tensor(split, raw, ws.to_broadcast([P, CH * H, CF]), ALU.mult)\
                            .then_inc(S["s_made"], 1)
                        dve.wait_ge(S["s_made"], i + 1)
                        nc.vector.tensor_copy(parts[:, :, 0, :], split).then_inc(S["s_chain"], 1)
                        dve.wait_ge(S["s_chain"], 3 * i + 1)
                        nc.vector.tensor_tensor(split, split, parts[:, :, 0, :], ALU.subtract)\
                            .then_inc(S["s_chain"], 1)
                    if 1 in halves:
                        dve.wait_ge(S["s_chain"], 3 * i + 2)
                        nc.vector.tensor_copy(parts[:, :, 1, :], split).then_inc(S["s_chain"], 1)
                        dve.wait_ge(S["s_chain"], 3 * i + 3)
                        nc.vector.tensor_tensor(parts[:, :, 2, :], split, parts[:, :, 1, :], ALU.subtract)\
                            .then_inc(S["sw_ready"], 1)

                def high(t):
                    dve.wait_ge(S["n_made"], NC * (ph - 1) + (t + 1))
                    nc.vector.tensor_copy(Sv[:, CH * t:CH * t + CH, :, 0, :].rearrange("p j h e -> p (j h) e"),
                                          S1[:, CH * t:CH * t + CH, :]
                                          .rearrange("p j (h e) -> p (j h) e", h=H)[:, :, 0:CF])\
                        .then_inc(S["n_high"], 1)

                both = kind == "AB"
                if kind == "A":
                    for t in range(NC):
                        statistics0(t)
                else:
                    if both:
                        statistics0(0)
                        statistics0(1)
                    move_features(0)
                    move_features(1)
                    if both:
                        statistics0(2)
                    move_features(2)
                    if both:
                        statistics0(3)
                    move_features(3)
                    maxima(1)
                    shifted(1)
                    split_features(0)
                    mean(1)
                    for t in range(1, NC - 1):
                        split_features(t)
                        high(t - 1)
                    split_features(NC - 1, [0])
                    high(NC - 2)
                    if not both:
                        split_features(NC - 1, [1])
                        high(NC - 1)
                if kind != "B":
                    maxima(0)
                    shifted(0)
                    mean(0)
                    if both:
                        split_features(NC - 1, [1])
                        high(NC - 1)
                    wait_alone(dve, S["misc_used"], misc_before_layer(kind, ph, 0) + 3)

            def steps(kind, events, ph, c):
                n = ph * NC + c
                vec, act_ = compared(kind)
                before = compares_before(kind, n)
                for e in vector_order(kind, events):
                    if e[0] == "A":
                        j = e[1]
                        if j == 0:
                            dve.wait_ge(S["misc_used"], rb_for(kind, ph, c, H if kind != "A" else 0))
                            dve.wait_ge(S["mask_ready"], 2 * CH * n + 2 * CH)
                        if j % 2 == 0:
                            dve.wait_ge(S["tile_free"], NJ * n + (j + 2))
                        nc.vector.scalar_tensor_tensor(out=tiles[:, j % RING, :], in0=Rb[:, H, :],
                                                       scalar=w[0][:, j, :], in1=mask[:, n % MSLOTS, j, :],
                                                       op0=ALU.max, op1=ALU.mult).then_inc(S["tile_ready"], 1)
                        continue
                    if e[0] == "MEAN":
                        for k in range(CH):
                            xk = xb[:, (n + NC) % XSLOTS, k, :].rearrange("p (h c) -> p h c", h=H)
                            last = nc.vector.scalar_tensor_tensor(
                                out=xk, in0=mean_h[1][:, :].rearrange("p (h e) -> p h e", h=H)[:, :, 0:C],
                                scalar=alone[:, c, k:k + 1], in1=xk, op0=ALU.mult, op1=ALU.add)
                        last.then_inc(S["mean_added"], 1)
                        continue
                    if e[0] == "X1":
                        n1, c1 = n - e[1], c - e[1]
                        if kind != "A":
                            dve.wait_ge(S["mean_added"], n - (NC - 1))
                        dve.wait_ge(S["a_moved"], n1 + 2)
                        nc.vector.tensor_scalar(alone_now[:, :], numA[:, :, F], 0.0, None, ALU.is_equal)
                        nc.vector.tensor_scalar(alone[:, c1, :], numA[:, :, F], 0.0, None, ALU.is_equal)
                        nc.vector.tensor_scalar(denA[:, :], numA[:, :, F], TINY, None, ALU.max)\
                            .then_inc(S["a_den"], 1)
                        dve.wait_ge(S["a_den"], n1 + 1)
                        nc.vector.reciprocal(denA[:, :], denA[:, :]).then_inc(S["a_rec"], 1)
                        xs = xb[:, n1 % XSLOTS, :, :]
                        for k in range(CH):
                            last = nc.vector.scalar_tensor_tensor(
                                out=xs[:, k, :], in0=mean_h[0][:, 0:F], scalar=alone_now[:, k:k + 1],
                                in1=xs[:, k, :], op0=ALU.mult, op1=ALU.add)
                        last.then_inc(S["a_sum"], 1)
                        dve.wait_ge(S["a_rec"], n1 + 1)
                        dve.wait_ge(S["a_sum"], n1 + 1)
                        for k in range(CH):
                            last = nc.vector.scalar_tensor_tensor(
                                out=xs[:, k, :], in0=numA[:, k, 0:F], scalar=denA[:, k:k + 1],
                                in1=xs[:, k, :], op0=ALU.mult, op1=ALU.add)
                        last.then_inc(S["x1_ready"], 1)
                        dve.wait_ge(S["x1_ready"], n1 + 2)
                        mean_variance(1, n1, 2, n1 + 1)
                        continue
                    if e[0] == "C0":
                        h, g = e[1:]
                        dve.wait_ge(S["misc_used"], rb_for(kind, ph, c, h))
                        for jj in range(JG):
                            last = nc.vector.tensor_scalar(c0[:, jj, :], Rb[:, h, :],
                                                           w[1][:, JG * g + jj, h:h + 1], 255.0, ALU.is_gt, ALU.mult)
                        last.then_inc(S["c0_ready"], 1)
                        continue
                    h, g = e[1:]
                    slot = g % BRING
                    chunk_mask = mask[:, (n - NC) % MSLOTS, JG * g:JG * g + JG, :].bitcast(u32)
                    n_bits, s_bits = bits[:, slot, 0, :, :].bitcast(u32), bits[:, slot, 1, :, :].bitcast(u32)
                    i = G * h + g
                    if e[0] == "N":
                        if i in vec:
                            dve.wait_ge(S["c0_ready"], before[0] + (vec.index(i) + 1))
                            src = c0[:, :, :]
                        else:
                            dve.wait_ge(S["c_ready"], before[1] + (act_.index(i) + 1))
                            src = cmp[:, act_.index(i) % CRING, :, :]
                        dve.wait_ge(S["bits_free"], HG * (n - NC) + (i + 1))
                        if i < BRING:
                            wait_alone(dve, S["sv_ready"], NC * (ph - 1) + (i + 1))
                        nc.vector.tensor_tensor(n_bits, src.bitcast(u32), chunk_mask, ALU.bitwise_and)\
                            .then_inc(S["n_ready"], 1)
                    else:
                        dve.wait_ge(S["n_ready"], HG * (n - NC) + (NR + i + 1))
                        nc.vector.tensor_tensor(s_bits, n_bits, chunk_mask, ALU.bitwise_xor)\
                            .then_inc(S["bits_ready"], 1)

            phases(dve, features, steps)


def kernel(x, adj, L0_gnn_W, L0_gnn_a_src, L0_gnn_a_dst, L1_gnn_W, L1_gnn_b, L1_gnn_a):
    import numpy as np
    import concourse.bacc as bacc
    from concourse.bass_utils import run_bass_kernel_spmd

    nc = bacc.Bacc("TRN2", target_bir_lowering=False, num_devices=1)
    given = dict(x=x, adj=adj, W0=L0_gnn_W, a0_src=L0_gnn_a_src, a0_dst=L0_gnn_a_dst,
                 W1=L1_gnn_W, b1=L1_gnn_b, a1=L1_gnn_a)
    arrays = {f"in_{name}": np.ascontiguousarray(a) for name, a in given.items()}
    args = [nc.dram_tensor(name, a.shape, mybir.dt.from_np(a.dtype), kind="ExternalInput").ap()
            for name, a in arrays.items()]
    out = nc.dram_tensor("out", arrays["in_x"].shape, mybir.dt.float32, kind="ExternalOutput").ap()
    gat_two_layers(nc, *args, out)
    return run_bass_kernel_spmd(nc, [arrays], core_ids=[0]).results[0]["out"]
```
